# Optimizing a Trainium2 kernel written in Bass

```python
import numpy as np
import jax
import jax.numpy as jnp

def _softmax(x, axis=-1):
    return jax.nn.softmax(x, axis=axis)

def _gelu(x):
    return jax.nn.gelu(x, approximate=True)

def _silu(x):
    return jax.nn.silu(x)

def _sigmoid(x):
    return jax.nn.sigmoid(x)

def _layernorm(x, axis=-1, eps=1e-05):
    m = jnp.mean(x, axis=axis, keepdims=True)
    v = jnp.var(x, axis=axis, keepdims=True)
    return (x - m) / jnp.sqrt(v + eps)

def _scatter_add(tgt, idx, src, axis=0):
    return tgt.at[idx].add(src)

def _segment_sum(src, seg, n):
    return jax.ops.segment_sum(src, seg, n)
kernel_name = 'mk_adj_ffn_d1_adj_r2_523dc9'

def setup_inputs(seed: int=0):
    np.random.seed(seed)
    _w = jnp.asarray

    def _rec_inputs():
        import jax
        import jax.numpy as jnp
        _gk = jax.random.key(seed)
        x = -0.0002928 + 1 * jax.random.normal(jax.random.fold_in(_gk, 1), (2048, 256), jnp.float32)
        _a = jax.random.bernoulli(jax.random.fold_in(_gk, 2), 0.0078125, (2048, 2048))
        _a = jnp.logical_or(_a, jnp.swapaxes(_a, -1, -2))
        _a = jnp.logical_or(_a, jnp.eye(2048, dtype=bool))
        _af = _a.astype(jnp.float32)
        _af = _af / jnp.maximum(_af.sum(-1, keepdims=True), 1.0)
        adj = _af
        return (x, adj)
    x, adj = _rec_inputs()

    def _L0_gnn_setup():
        import jax, jax.numpy as jnp
        import numpy as np
        N = 4096
        D = 256
        H = 256

        def _graph_conv(feats, adj, W, b):
            agg = adj @ feats
            cat = jnp.concatenate([feats, agg], axis=-1)
            return jax.nn.relu(jnp.einsum('nd,df->nf', cat, W) + b)
        key = jax.random.key(seed)
        k1, k2, k3, k4 = jax.random.split(key, 4)
        x = jax.random.normal(k1, (N, D), dtype=jnp.float32)
        adj = jax.random.uniform(k2, (N, N), dtype=jnp.float32)
        adj = adj / jnp.sum(adj, axis=-1, keepdims=True)
        lim1 = float(np.sqrt(6.0 / (2 * D + H)))
        lim2 = float(np.sqrt(6.0 / (2 * H + H)))
        W1 = jax.random.uniform(k3, (2 * D, H), dtype=jnp.float32, minval=-lim1, maxval=lim1)
        W2 = jax.random.uniform(k4, (2 * H, H), dtype=jnp.float32, minval=-lim2, maxval=lim2)
        b1 = jnp.zeros((H,), dtype=jnp.float32)
        b2 = jnp.zeros((H,), dtype=jnp.float32)
        return {'x': x, 'adj': adj, 'W1': W1, 'b1': b1, 'W2': W2, 'b2': b2}
    _L0_gnn_all = _L0_gnn_setup()
    _L0_gnn_in = {k: v for k, v in _L0_gnn_all.items() if k in ('W1', 'b1', 'W2', 'b2')}
    del _L0_gnn_all

    def _L0_ffn_setup():
        import jax, jax.numpy as jnp
        import numpy as np
        NUM_EXPERTS = 8
        TOP_K = 2
        key = jax.random.key(seed)
        ks = jax.random.split(key, 6)
        B, S, D, F, E = (2, 1024, 256, 768, NUM_EXPERTS)
        scale = 0.02
        return {'x': jax.random.normal(ks[0], (B, S, D), dtype=jnp.float32), 'Wg': jax.random.normal(ks[1], (D, E), dtype=jnp.float32) * scale, 'W1': jax.random.normal(ks[2], (E, D, F), dtype=jnp.float32) * scale, 'W2': jax.random.normal(ks[3], (E, F, D), dtype=jnp.float32) * scale, 'W3': jax.random.normal(ks[4], (E, D, F), dtype=jnp.float32) * scale, 'b3': jax.random.normal(ks[5], (E, F), dtype=jnp.float32) * scale}
    _L0_ffn_all = _L0_ffn_setup()
    _L0_ffn_in = {k: v for k, v in _L0_ffn_all.items() if k in ('Wg', 'W1', 'W2', 'W3', 'b3')}
    del _L0_ffn_all
    return {'x': x, 'adj': adj, 'L0_gnn_W1': _L0_gnn_in['W1'], 'L0_gnn_b1': _L0_gnn_in['b1'], 'L0_gnn_W2': _L0_gnn_in['W2'], 'L0_gnn_b2': _L0_gnn_in['b2'], 'L0_ffn_Wg': _L0_ffn_in['Wg'], 'L0_ffn_W1': _L0_ffn_in['W1'], 'L0_ffn_W2': _L0_ffn_in['W2'], 'L0_ffn_W3': _L0_ffn_in['W3'], 'L0_ffn_b3': _L0_ffn_in['b3']}

def reference(x, adj, L0_gnn_W1, L0_gnn_b1, L0_gnn_W2, L0_gnn_b2, L0_ffn_Wg, L0_ffn_W1, L0_ffn_W2, L0_ffn_W3, L0_ffn_b3):
    import jax
    import jax.numpy as jnp

    def _L0_gnn_ref(x, adj, W1, b1, W2, b2):
        import jax, jax.numpy as jnp
        import numpy as np
        N = 4096
        D = 256
        H = 256

        def _graph_conv(feats, adj, W, b):
            agg = adj @ feats
            cat = jnp.concatenate([feats, agg], axis=-1)
            return jax.nn.relu(jnp.einsum('nd,df->nf', cat, W) + b)
        h = _graph_conv(x, adj, W1, b1)
        out = jax.nn.relu(_graph_conv(h, adj, W2, b2) + h)
        return out

    def _L0_ffn_ref(x, Wg, W1, W2, W3, b3):
        import jax, jax.numpy as jnp
        import numpy as np
        NUM_EXPERTS = 8
        TOP_K = 2
        logits = jnp.einsum('bsd,de->bse', x, Wg)
        top_logits, top_idx = jax.lax.top_k(logits, TOP_K)
        top_w = jax.nn.softmax(top_logits, axis=-1)
        onehot = jax.nn.one_hot(top_idx, NUM_EXPERTS, dtype=x.dtype)
        C = jnp.sum(onehot * top_w[..., None], axis=-2)
        h = jnp.einsum('bsd,edf->bsef', x, W1)
        g = jnp.einsum('bsd,edf->bsef', x, W3) + b3
        act = jax.nn.silu(h) * g
        out = jnp.einsum('bse,bsef,efd->bsd', C, act, W2)
        return out
    x = x + _L0_gnn_ref(_layernorm(x, axis=-1), adj, L0_gnn_W1, L0_gnn_b1, L0_gnn_W2, L0_gnn_b2)
    x = x + _L0_ffn_ref(_layernorm(x, axis=-1)[None], L0_ffn_Wg, L0_ffn_W1, L0_ffn_W2, L0_ffn_W3, L0_ffn_b3)[0]
    return x

_drawn_inputs = setup_inputs


def setup_inputs(seed=0):
    import zlib

    import numpy as np

    out = dict(_drawn_inputs(seed))
    spreads = {'L0_gnn_b1': (0.0, 0.1), 'L0_gnn_b2': (0.0, 0.1)}
    factors = {'L0_ffn_Wg': 3.971,
     'L0_ffn_W1': 3.505,
     'L0_ffn_W2': 3.469,
     'L0_ffn_W3': 3.469,
     'L0_ffn_b3': 8.0}
    for name, (base, spread) in spreads.items():
        noise = np.random.default_rng([zlib.crc32(name.encode()), seed]).standard_normal(out[name].shape)
        drawn = base * np.exp(spread * noise) if base else spread * noise
        out[name] = jnp.asarray(drawn.astype(out[name].dtype))
    for name, factor in factors.items():
        out[name] = (out[name] * factor).astype(out[name].dtype)
    return out
```

```python
from contextlib import ExitStack

import concourse.bass as bass
from concourse import mybir

P = 128
F32, F16 = mybir.dt.float32, mybir.dt.float16
I32, U32 = mybir.dt.int32, mybir.dt.uint32
ALU = mybir.AluOpType
ACT = mybir.ActivationFunctionType
AX_X = mybir.AxisListType.X

S_ACT = 16.0
S_W = 1024.0
S_SUM = S_ACT * S_W
EPS = 1e-5
HI, LO = 0, 1
PASSES = ((HI, HI), (LO, HI), (HI, LO))
TOP = 2


class Steps:

    def __init__(self, eng, sem):
        self.eng, self.sem, self.base, self.n = eng, sem, 0, 0

    def wait_for(self, ins):
        self.n += 1
        ins.then_inc(self.sem, 1)
        self.eng.wait_ge(self.sem, self.base + self.n)


def moe_gnn_kernel(nc, x, adj, gnn_w1, gnn_b1, gnn_w2, gnn_b2, wg, w1, w2, w3, b3, out):
    N, D = x.shape
    E, _, F = w1.shape
    NT, KD, KF = N // P, D // P, F // P
    CW = 512
    NC, TPC = N // CW, CW // P
    JB = CW // P
    GPC = TPC * NT // JB
    GPR = GPC // TPC
    NP = 3
    FP = F // NP
    ROW = D + 2
    REG = N + P
    TILES = TOP * N // P + E - 1
    UN = 3
    W13 = 2 * KD * NP * CW
    EW = W13 + 2 * KF * D
    ADJC = 2 * NT * CW
    EXT = E * EW - NC * ADJC
    PIECES = 2 * KD + 2
    SLOTS = 3
    assert 2 * FP == CW and NC == 4 and TPC == 4 and EXT == 4 * N and EW <= ADJC
    assert TILES % UN == 0 and KF == 2 * NP and GPC == NT and E == 2 * NC
    assert PIECES % SLOTS == 0

    routed = nc.dram_tensor("routed_rows", (E * REG, ROW), F32, kind="Internal").ap()
    total = nc.dram_tensor("row_sums", (N + P, D), F32, kind="Internal").ap()
    x_t = x.rearrange("(t p) d -> p t d", p=P)
    total_t = total.rearrange("(t p) d -> p t d", p=P)

    with ExitStack() as ctx:
        def sb(name, shape, dt):
            return ctx.enter_context(nc.sbuf_tensor(name, shape, dt))

        def sem(name):
            return ctx.enter_context(nc.semaphore(name))

        big = sb("big", [P, E * EW], F16)
        tu = sb("tu", [P, 2 * KD * N + 2 * NT * D], F16)
        rb = sb("rb", [P, 2 * N], F32)
        gw = sb("gw", [P, 2 * 2 * 2 * KD * D], F16)
        stage = sb("stage", [P, 2, F], F32)
        ident = sb("ident", [P, P], F32)
        before = sb("before", [P, P], F16)
        ones = sb("ones", [P, P], F16)
        fixed = sb("fixed", [P, 76], F32)
        bias = fixed[:, 0:4].rearrange("p (l k) -> p l k", l=2)
        bias_h = fixed[:, 4:6]
        wg_sb = fixed[:, 6:6 + KD * E].rearrange("p (k e) -> p k e", k=KD)
        eps = fixed[:, 22:23]
        scratch = fixed[:, 23:24]
        iota_e = fixed[:, 24:32]
        region_0 = fixed[:, 32:40]
        token_no = fixed[:, 40:56]
        token_w = fixed[:, 56:56 + UN]
        token_ix = fixed[:, 60:60 + UN].bitcast(U32)
        rstd_2 = fixed[:, 64:68]
        std_2 = fixed[:, 68:72]
        carry = fixed[:, 72:76].bitcast(F16)

        adj_t = big[:, EXT:].rearrange("p (c h j w) -> p c h j w", c=NC, h=2, j=NT)
        low_rows = big[:, 0:EXT].bitcast(F32)
        adj_rows = [low_rows[:, 0:N], low_rows[:, N:2 * N], rb[:, 0:N], rb[:, N:2 * N]]
        late = EXT + (NC - 1) * ADJC
        x_all = big[:, late:late + ADJC // 2].bitcast(F32).rearrange("p (t d) -> p t d", t=NT)
        xn_all = big[:, late + ADJC // 2:].bitcast(F32).rearrange("p (t d) -> p t d", t=NT)
        raw = big[:, late - ADJC:late].bitcast(F32)
        gw_raw = raw[:, 0:4 * KD * D]
        st_1 = raw[:, 4 * KD * D:4 * KD * D + 6 * NT].rearrange("p (t s) -> p t s", t=NT)
        mv_1 = raw[:, 4 * KD * D + 128:4 * KD * D + 128 + 2 * NT].rearrange("p (t s) -> p t s", t=NT)
        std_1 = raw[:, 4 * KD * D + 160:4 * KD * D + 160 + NT]
        rstd_1 = raw[:, 4 * KD * D + 176:4 * KD * D + 176 + NT]
        act_t = tu[:, 0:2 * KD * N].rearrange("p (c h k w) -> p c h k w", c=NC, h=2, k=KD)
        u = tu[:, 2 * KD * N:].rearrange("p (h j d) -> p h j d", h=2, j=NT)
        gwp = gw[:, :].rearrange("p (l h k d) -> p l h k d", l=2, h=2, k=2 * KD)
        sum_1 = stage[:, :, 0:CW]
        arriving = [stage[:, 0, :], stage[:, 1, :], tu[:, 0:2 * F].bitcast(F32)]
        sum_2 = gw[:, 0:2 * 2 * KD * D].bitcast(F32).rearrange("p (f w) -> p f w", f=KD)
        xn2_t = gw[:, 0:2 * 2 * KD * D].bitcast(F32)

        y_ch = rb[:, 0:TPC * D].rearrange("p (q d) -> p q d", q=TPC)
        at = TPC * D
        row = []
        for k in range(TOP):
            row.append(rb[:, at:at + TPC * ROW].rearrange("p (q d) -> p q d", q=TPC))
            at += TPC * ROW
        small = {}
        for name, n in (("st_2", 24), ("mv_2", 8), ("logits", 32), ("best", 32), ("best_ix", 32),
                        ("choice", 8), ("onehot", 64), ("place", 32), ("picked", 64),
                        ("slot_f", 8), ("slot", 8), ("gap", 4), ("expd", 4), ("den", 4),
                        ("mask", 16), ("added", 4)):
            small[name] = rb[:, at:at + n]
            at += n
        st_2 = small["st_2"].rearrange("p (q s) -> p q s", q=TPC)
        mv_2 = small["mv_2"].rearrange("p (q s) -> p q s", q=TPC)
        logits = small["logits"].rearrange("p (q e) -> p q e", q=TPC)
        best = small["best"].rearrange("p (q e) -> p q e", q=TPC)
        best_ix = small["best_ix"].bitcast(U32).rearrange("p (q e) -> p q e", q=TPC)
        choice = small["choice"].rearrange("p (q k) -> p q k", q=TPC)
        onehot = small["onehot"].rearrange("p (q k e) -> p q k e", q=TPC, k=TOP)
        picked = small["picked"].rearrange("p (q k e) -> p q k e", q=TPC, k=TOP)
        place = small["place"].rearrange("p (q e) -> p q e", q=TPC)
        slot_f, slot = small["slot_f"], small["slot"].bitcast(U32)
        gap, expd, den = small["gap"], small["expd"], small["den"]
        mask = small["mask"].bitcast(F16).rearrange("p (q e) -> p q e", q=TPC)
        added = small["added"].bitcast(F16)
        iota_k = rb[0:1, at:at + NT]
        upto = rb[0:1, at + 16:at + 80].rearrange("p (a b) -> p a b", a=E)
        iota_n = rb[0:1, at + 80:at + 80 + TILES]
        cnt = rb[0:1, at + 120:at + 120 + 8 * E]
        n_e, nt_e, last, first, delta, pad_f = (cnt[:, E * i:E * i + E] for i in range(6))
        pad_row = cnt[:, 6 * E:7 * E].bitcast(I32)
        experts_seen = rb[0:1, at + 184:at + 184 + TILES]
        row_shift = rb[0:1, at + 224:at + 224 + TILES]
        tab_f = rb[0:1, at + 264:at + 264 + 3 * TILES].rearrange("p (a t) -> p a t", a=3)
        assert at + 264 + 3 * TILES <= 2 * N
        wide = gw[0:1, 0:4 * KD * D].bitcast(F32)
        over_k = wide[:, 0:E * NT].rearrange("p (e k) -> p e k", e=E)
        over_e = wide[:, 128:128 + E * E].rearrange("p (a b) -> p a b", a=E)
        started = wide[:, 192:192 + E * TILES].rearrange("p (t e) -> p t e", e=E)
        shifts = wide[:, 512:512 + E * TILES].rearrange("p (t e) -> p t e", e=E)
        gw_2 = gw[:, 4 * KD * D:]
        x_in = gw_2[:, 0:2 * UN * ROW].bitcast(F32).rearrange("p (s d) -> p s d", s=UN)
        table = gw_2[0:1, 2 * UN * ROW:2 * UN * ROW + 6 * TILES].bitcast(I32).rearrange(
            "p (a t) -> p a t", a=3)

        b3_all = tu[:, 2 * F:2 * F + 2 * E * F].bitcast(F32)
        free = 2 * F + 2 * E * F
        b3_early = ((NC - 1) * 2 * KD * CW - 2 * F) // (2 * F)
        pad = tu[:, free:free + 2 * ROW].bitcast(F32)
        free += 2 * ROW
        x_part = tu[:, free:free + 2 * D].rearrange("p (h d) -> p h d", h=2)
        silu_h, gated, act_f = (rb[:, F * i:F * i + F] for i in range(3))
        act_part = rb[:, 3 * F:4 * F].bitcast(F16).rearrange("p (h f) -> p h f", h=2)
        y_out = rb[:, 4 * F:4 * F + UN * D].rearrange("p (s d) -> p s d", s=UN)

        psum = ctx.enter_context(nc.psum_tensor("psum", [P, 8, CW], F32))
        SUM = (0, 1)
        TP = (2, 3, 4, 5)
        UB = (6, 7)
        OT, XT, GATE, COUNT = (2, 3), (4, 5), 6, 7
        FA, FX, FY = (3, 4), 5, 6

        small_in, gw_in = sem("small_in"), sem("gw_in")
        x_arrived = [sem(f"x_arrived{c}") for c in range(NC)]
        row_arrived = [sem(f"row_arrived{r}") for r in range(TPC)]
        piece_arrived = [sem(f"piece_arrived{s}") for s in range(SLOTS)]
        xin_arrived = [sem(f"xin_arrived{s}") for s in range(UN)]
        consts, zeroed, late_consts = sem("consts"), sem("zeroed"), sem("late_consts")
        dve_step, pool_step = sem("dve_step"), sem("pool_step")
        var_1, std_1_ready, xn_ready, bias_ready = sem("var_1"), sem("std_1_ready"), sem("xn_ready"), sem("bias_ready")
        gw_hi, gw_lo = sem("gw_hi"), sem("gw_lo")
        xt_tp, xt_hi, xt_lo = sem("xt_tp"), sem("xt_hi"), sem("xt_lo")
        u_mm, u_hi, u_lo = sem("u_mm"), sem("u_hi"), sem("u_lo")
        adj_tp, adj_hi, adj_lo = sem("adj_tp"), sem("adj_hi"), sem("adj_lo")
        sum_mm, sum_read, h_parts, o_ready = sem("sum_mm"), sem("sum_read"), sem("h_parts"), sem("o_ready")
        o_tp, x_again, y_ready, y_stored = sem("o_tp"), sem("x_again"), sem("y_ready"), sem("y_stored")
        var_2, std_2_ready, row_ready = sem("var_2"), sem("std_2_ready"), sem("row_ready")
        row_copied = sem("row_copied")
        xn2_tp, xn2_copied, logits_mm = sem("xn2_tp"), sem("xn2_copied"), sem("logits_mm")
        gap_ready, exp_ready, mask_ready, rank_mm = sem("gap_ready"), sem("exp_ready"), sem("mask_ready"), sem("rank_mm")
        gate_read, slots_ready, weights_ready = sem("gate_read"), sem("slots_ready"), sem("weights_ready")
        scattered, carried = sem("scattered"), sem("carried")
        piece_hi, piece_lo = sem("piece_hi"), sem("piece_lo")
        count_mm, pads_known, table_ready = sem("count_mm"), sem("pads_known"), sem("table_ready")
        pad_built, pad_stored, b3_arrived = sem("pad_built"), sem("pad_stored"), sem("b3_arrived")
        b3_early_in = sem("b3_early_in")
        token_read = sem("token_read")
        fx_tp, fx_hi, fx_lo = sem("fx_tp"), sem("fx_hi"), sem("fx_lo")
        hg_mm, silu_ready, gated_ready, act_ready = sem("hg_mm"), sem("silu_ready"), sem("gated_ready"), sem("act_ready")
        fa_tp, fa_hi, fa_lo = sem("fa_tp"), sem("fa_hi"), sem("fa_lo")
        fy_mm, fy_ready, fy_added, out_stored = sem("fy_mm"), sem("fy_ready"), sem("fy_added"), sem("out_stored")

        def ffn_tiles(eng, first_tile, tile, last_tile):
            first_tile()
            for t in range(1, UN):
                tile(t, t, 0, True, True)
            with eng.Fori(1, TILES // UN - 1) as i:
                for s in range(UN):
                    tile(i * UN + s, s, i, True, False)
            for t in range(TILES - UN, TILES):
                tile(t, t % UN, t // UN, t < TILES - 1, False)
            last_tile(TILES - 1, (TILES - 1) % UN)

        def expert_piece(e, n, part):
            mine = big[:, bass.ds(e * EW, EW)]
            if n < 2 * KD:
                v = mine[:, 0:W13].rearrange("p (k h m w) -> p k h m w", k=KD, h=2, m=NP)
                side = n // KD
                return v[:, n % KD, part, :, side * FP:(side + 1) * FP]
            v = mine[:, W13:].rearrange("p (f h d) -> p f h d", f=KF, h=2)
            half = n - 2 * KD
            return v[:, NP * half:NP * (half + 1), part, :]

        def acts(c, part, k):
            return act_t[:, bass.ds(c, 1), part, k, :].rearrange("p a w -> p (a w)")

        block = ctx.enter_context(nc.Block())

        @block.sync
        def _(sp):
            for c in range(2):
                sp.dma_start(x_all[:, TPC * c:TPC * (c + 1), :], x_t[:, TPC * c:TPC * (c + 1), :]
                             ).then_inc(x_arrived[c], 16)
            for r in range(TPC):
                sp.dma_start(adj_rows[r], adj[r * P:(r + 1) * P, :]).then_inc(row_arrived[r], 16)
            with sp.Fori(1, NC) as c:
                for r in range(TPC):
                    sp.wait_ge(adj_tp, (c - 1) * GPC + (r + 1) * GPR)
                    sp.dma_start(adj_rows[r], adj[bass.ds((c * TPC + r) * P, P), :]
                                 ).then_inc(row_arrived[r], 16)

            def load_piece(e, n):
                if n < 2 * KD:
                    w, k = (w1, w3)[n // KD], n % KD
                    src = w[bass.ds(e, 1), k * P:(k + 1) * P, :].rearrange("a p f -> (a p) f")
                    dst = arriving[n % SLOTS]
                else:
                    h = n - 2 * KD
                    src = w2[bass.ds(e, 1), h * NP * P:(h + 1) * NP * P, :].rearrange(
                        "a (f p) d -> (a p) f d", p=P)
                    dst = arriving[n % SLOTS].rearrange("p (f d) -> p f d", f=NP)
                sp.dma_start(dst, src).then_inc(piece_arrived[n % SLOTS], 16)

            sp.wait_ge(h_parts, KD * NC)
            for n in range(PIECES):
                if n == SLOTS - 1:
                    sp.wait_ge(o_ready, KD)
                if n >= SLOTS:
                    sp.wait_ge(piece_lo, n + 1 - SLOTS)
                load_piece(0, n)
            with sp.Fori(1, E - 1) as e:
                for n in range(PIECES):
                    sp.wait_ge(piece_lo, e * PIECES + (n + 1 - SLOTS))
                    load_piece(e, n)

            def load_last(n):
                sp.wait_ge(piece_lo, (E - 1) * PIECES + (n + 1 - SLOTS))
                load_piece(E - 1, n)

            def store_pad(e):
                end = sp.value_load(pad_row[:, e:e + 1], min_val=e * REG, max_val=e * REG + N)
                sp.dma_start(routed[bass.ds(end, P), :], pad[:, :]).then_inc(pad_stored, 16)

            for n in range(SLOTS):
                load_last(n)
            sp.wait_ge(pad_built, 1)
            sp.dma_start(total[N:N + P, :], pad[:, 0:D]).then_inc(pad_stored, 16)
            sp.wait_ge(pads_known, 1)
            for n in range(SLOTS, PIECES):
                store_pad(n - SLOTS)
                load_last(n)
            for e in range(PIECES - SLOTS, E):
                store_pad(e)
            sp.wait_ge(pad_stored, 16 * (E + 1))
            sp.wait_ge(scattered, 16 * NT * TOP)
            sp.wait_ge(y_stored, 16 * NC)
            sp.wait_ge(table_ready, 1)

            def load_tile(t, s):
                start = sp.value_load(table[:, 0, bass.ds(t, 1)], min_val=0, max_val=E * REG - P)
                sp.dma_start(x_in[:, s, :], routed[bass.ds(start, P), :]).then_inc(xin_arrived[s], 16)

            for t in range(UN):
                load_tile(t, t)
            with sp.Fori(1, TILES // UN) as i:
                for s in range(UN):
                    sp.wait_ge(fx_tp, (i - 1) * UN + (s + 1))
                    sp.wait_ge(token_read, (i - 1) * UN + (s + 1))
                    load_tile(i * UN + s, s)
            sp.wait_ge(fy_added, 16 * TILES)
            sp.dma_start(out, total[0:N, :]).then_inc(out_stored, 16)
            sp.wait_ge(out_stored, 16)

        @block.gpsimd
        def _(pool):
            step = Steps(pool, pool_step)
            nc.gpsimd.memset(ident[:], 0.0)
            nc.gpsimd.memset(ones[:], 1.0)
            nc.gpsimd.memset(carry, 0.0)
            nc.gpsimd.memset(eps, EPS)
            nc.gpsimd.iota(iota_e, pattern=[[1, E]], base=0, channel_multiplier=0,
                           allow_small_or_imprecise_dtypes=True)
            nc.gpsimd.iota(region_0, pattern=[[REG, E]], base=0, channel_multiplier=0,
                           allow_small_or_imprecise_dtypes=True)
            step.wait_for(nc.gpsimd.iota(token_no, pattern=[[P, NT]], base=0, channel_multiplier=1,
                                         allow_small_or_imprecise_dtypes=True))
            nc.gpsimd.affine_select(out=before[:], in_=ones[:], compare_op=ALU.is_gt, fill=0.0,
                                    base=0, pattern=[[1, P]], channel_multiplier=-1)
            nc.gpsimd.affine_select(out=ident[:], in_=ident[:], compare_op=ALU.not_equal, fill=1.0,
                                    base=0, pattern=[[-1, P]], channel_multiplier=1
                                    ).then_inc(consts, 1)
            pool.wait_ge(adj_tp, NC * GPC)
            nc.gpsimd.iota(iota_k, pattern=[[P, NT]], base=0, channel_multiplier=0,
                           allow_small_or_imprecise_dtypes=True)
            nc.gpsimd.iota(iota_n, pattern=[[1, TILES]], base=0, channel_multiplier=0,
                           allow_small_or_imprecise_dtypes=True)
            step.wait_for(nc.gpsimd.memset(upto, 1.0))
            nc.gpsimd.affine_select(out=upto, in_=upto, compare_op=ALU.is_ge, fill=0.0, base=0,
                                    pattern=[[1, E], [-1, E]], channel_multiplier=0
                                    ).then_inc(late_consts, 1)

            def scatter(c, first):
                if not first:
                    pool.wait_ge(scattered, c * (16 * TPC * TOP))
                for k in range(TOP):
                    ins = nc.gpsimd.tensor_copy(row[k][:, :, D + 1], token_no[:, bass.ds(c * TPC, TPC)])
                step.wait_for(ins)
                pool.wait_ge(row_copied, c + 1)
                pool.wait_ge(slots_ready, c + 1)
                pool.wait_ge(weights_ready, c + 1)
                for q in range(TPC):
                    for k in range(TOP):
                        i = q * TOP + k
                        nc.gpsimd.indirect_dma_start(
                            out=routed, out_offset=bass.IndirectOffsetOnAxis(ap=slot[:, i:i + 1], axis=0),
                            in_=row[k][:, q, :], in_offset=None).then_inc(scattered, 16)

            for c in range(NC - 1):
                scatter(c, c == 0)

            pool.wait_ge(o_ready, KD * (NC - 1))
            pool.dma_start(b3_all[:, 0:b3_early * F], b3[0:b3_early, :].rearrange("e f -> (e f)").partition_broadcast(P)
                           ).then_inc(b3_early_in, 16)

            pool.wait_ge(sum_mm, 2 * KD * NC)
            nc.gpsimd.iota(pad[:, D + 1:D + 2], pattern=[[0, 1]], base=N, channel_multiplier=1,
                           allow_small_or_imprecise_dtypes=True)
            nc.gpsimd.memset(pad[:, 0:D + 1], 0.0).then_inc(pad_built, 1)

            scatter(NC - 1, False)

            pool.wait_ge(y_stored, 16 * NC)
            pool.wait_ge(pad_stored, 16)
            for t in range(TILES):
                pool.wait_ge(fy_ready, t + 1)
                if t:
                    pool.wait_ge(fy_added, 16 * t)
                s = t % UN
                nc.gpsimd.indirect_dma_start(
                    out=total, out_offset=bass.IndirectOffsetOnAxis(ap=token_ix[:, s:s + 1], axis=0),
                    in_=y_out[:, s, :], in_offset=None, compute_op=ALU.add).then_inc(fy_added, 16)

        @block.tensor
        def _(pe):
            mm = nc.tensor.matmul
            pe.wait_ge(consts, 1)
            for c in range(NC):
                pe.wait_ge(xn_ready, c + 1)
                for k in range(KD):
                    n = KD * c + k
                    if n >= len(TP):
                        pe.wait_ge(xt_lo, n - len(TP) + 1)
                    for q in range(TPC):
                        last = nc.tensor.transpose(psum[:, TP[n % 4], q * P:(q + 1) * P],
                                                   xn_all[:, TPC * c + q, k * P:(k + 1) * P], ident[:])
                    last.then_inc(xt_tp, 1)

            def rows_times_w(layer):
                for n in range(NT // 2):
                    if layer == 0:
                        pe.wait_ge(xt_lo, KD * (n // 2 + 1))
                    else:
                        pe.wait_ge(h_parts, KD * (n // 2 + 1))
                    if layer or n >= 2:
                        pe.wait_ge(u_lo, layer * (NT // 2) + n - 1)
                    for j in range(2):
                        jt = 2 * n + j
                        for i, (k, (a, b)) in enumerate((k, ab) for k in range(KD) for ab in PASSES):
                            last = mm(psum[:, UB[n % 2], j * D:(j + 1) * D],
                                      acts(jt // TPC, a, k)[:, (jt % TPC) * P:(jt % TPC + 1) * P], gwp[:, layer, b, KD + k, :],
                                      start=(i == 0), stop=(i == 3 * KD - 1))
                    last.then_inc(u_mm, 1)

            def transpose_group(c, g, first):
                r, jq = g // GPR, g % GPR
                if jq == 0:
                    pe.wait_ge(row_arrived[r], 16 * c + 16)
                if first and g < 4:
                    pe.wait_ge(xt_lo, KD * NC - 4 + g + 1)
                else:
                    pe.wait_ge(adj_lo, c * GPC + (g - 3))
                for b in range(JB):
                    j = JB * jq + b
                    last = nc.tensor.transpose(psum[:, TP[g % 4], b * P:(b + 1) * P],
                                               adj_rows[r][:, j * P:(j + 1) * P], ident[:])
                last.then_inc(adj_tp, 1)

            def chunk(layer, c, first, between):
                g = layer * NC + c
                if layer == 0:
                    pe.wait_ge(gw_lo, 1)
                for f in range(KD):
                    if not first:
                        pe.wait_ge(sum_read, KD * g + (f + 1 - KD))
                    for k in range(KD):
                        for i, (a, b) in enumerate(PASSES):
                            mm(psum[:, SUM[f], :], gwp[:, layer, a, k, f * P:(f + 1) * P],
                               acts(c, b, k), start=(k == 0 and i == 0), stop=False)
                pe.wait_ge(u_lo, (layer + 1) * (NT // 2))
                if layer == 0:
                    pe.wait_ge(adj_lo, c * GPC + GPC)
                for f in range(KD):
                    for j in range(NT):
                        for i, (a, b) in enumerate(PASSES):
                            last = mm(psum[:, SUM[f], :], u[:, a, j, f * P:(f + 1) * P],
                                      adj_t[:, bass.ds(c, 1), b, j, :].rearrange("p a w -> p (a w)"),
                                      start=False, stop=(j == NT - 1 and i == 2))
                        if j == NT - 1:
                            last.then_inc(sum_mm, 1)
                        for work in between.get((f, j), ()):
                            work()

            rows_times_w(0)
            for g in range(GPC):
                transpose_group(0, g, True)

            def with_next(c):
                return {(i // (NT // KD * 2) * 0 + i // NT, i % NT): [lambda g=i // 2: transpose_group(c + 1, g, False)]
                        for i in range(0, KD * NT, 2)}

            chunk(0, 0, True, with_next(0))
            with pe.Fori(1, NC - 1) as c:
                chunk(0, c, False, with_next(c))
            chunk(0, NC - 1, False, {})
            rows_times_w(1)

            def o_back(c, first):
                pe.wait_ge(o_ready, KD * c + KD)
                for b in range(2):
                    if not first:
                        pe.wait_ge(y_ready, 2 * c + (b - 1))
                    for q in (2 * b, 2 * b + 1):
                        for f in range(KD):
                            at = (q % 2) * D + f * P
                            last = nc.tensor.transpose(psum[:, OT[b], at:at + P],
                                                       sum_2[:, f, q * P:(q + 1) * P], ident[:])
                    last.then_inc(o_tp, 1)

            def xn2_transposes(c):
                for b in range(2):
                    pe.wait_ge(row_ready, 2 * c + (b + 1))
                    for q in (2 * b, 2 * b + 1):
                        for k in range(KD):
                            at = (q % 2) * D + k * P
                            last = nc.tensor.transpose(psum[:, XT[b], at:at + P],
                                                       row[0][:, q, k * P:(k + 1) * P], ident[:])
                    last.then_inc(xn2_tp, 1)

            def gate_logits(c, first):
                if not first:
                    pe.wait_ge(gate_read, c)
                for q in range(TPC):
                    if q % 2 == 0:
                        pe.wait_ge(xn2_copied, 2 * c + (q // 2 + 1))
                    for k in range(KD):
                        last = mm(psum[:, GATE, q * E:(q + 1) * E], xn2_t[:, (q * KD + k) * P:(q * KD + k + 1) * P],
                                  wg_sb[:, k, :], start=(k == 0), stop=(k == KD - 1))
                last.then_inc(logits_mm, 1)

            def ranks(c):
                pe.wait_ge(mask_ready, c + 1)
                o = psum[:, GATE, 64:64 + TPC * E].rearrange("p (q e) -> p q e", q=TPC)
                mm(o, before[:], mask, start=True, stop=False)
                mm(o, ones[:], carry.unsqueeze(1).to_broadcast([P, TPC, E]), start=False, stop=False)
                for d in range(1, TPC):
                    last = mm(o[:, d:, :], ones[:], mask[:, 0:TPC - d, :], start=False, stop=(d == TPC - 1))
                last.then_inc(rank_mm, 1)

            def tail(c, first):
                return {(0, 0): [lambda: o_back(c, first)],
                        (0, 13): [lambda: xn2_transposes(c)],
                        (1, 1): [lambda: gate_logits(c, first)],
                        (1, 8): [lambda: ranks(c)]}

            chunk(1, 0, False, {})
            chunk(1, 1, False, tail(0, True))
            with pe.Fori(2, NC) as c:
                chunk(1, c, False, tail(c - 1, False))
            o_back(NC - 1, False)
            xn2_transposes(NC - 1)
            gate_logits(NC - 1, False)
            ranks(NC - 1)
            pe.wait_ge(carried, NC)
            mm(psum[:, COUNT, 0:E], ones[:], carry, start=True, stop=True).then_inc(count_mm, 1)

            def x_transposes(t, s, nth, first=False):
                pe.wait_ge(xin_arrived[s], 16 * nth + 16)
                if not first:
                    pe.wait_ge(fx_lo, t)
                for k in range(KD):
                    last = nc.tensor.transpose(psum[:, FX, k * P:(k + 1) * P],
                                               x_in[:, s, k * P:(k + 1) * P], ident[:])
                last.then_inc(fx_tp, 1)

            def hidden(t, place, m, first=False):
                if m == 0:
                    pe.wait_ge(fx_lo, t + 1)
                    if not first:
                        pe.wait_ge(silu_ready, t)
                        pe.wait_ge(gated_ready, t)
                n = 0
                for k in range(KD):
                    for b, parts in ((HI, (HI, LO)), (LO, (HI,))):
                        w = big[:, bass.ds(place + ((k * 2 + b) * NP + m) * CW, CW)]
                        for a in parts:
                            last = mm(psum[:, m, :], x_part[:, a, k * P:(k + 1) * P], w,
                                      start=(n == 0), stop=(n == 3 * KD - 1))
                            n += 1
                if m == NP - 1:
                    last.then_inc(hg_mm, 1)

            def act_transposes(t, first=False):
                pe.wait_ge(act_ready, t + 1)
                for b, fs in enumerate((range(0, 4), range(4, KF))):
                    if not first:
                        pe.wait_ge(fa_lo, 2 * t + (b - 1))
                    for f in fs:
                        last = nc.tensor.transpose(psum[:, FA[b], (f % 4) * P:(f % 4 + 1) * P],
                                                   act_f[:, f * P:(f + 1) * P], ident[:])
                    last.then_inc(fa_tp, 1)

            def down(t, place, first=False):
                if not first:
                    pe.wait_ge(fy_ready, t)
                n = 0
                for f in range(KF):
                    if f == 0:
                        pe.wait_ge(fa_lo, 2 * t + 1)
                    if f == 4:
                        pe.wait_ge(fa_lo, 2 * t + 2)
                    for b, parts in ((HI, (HI, LO)), (LO, (HI,))):
                        w = big[:, bass.ds(place + (W13 + (f * 2 + b) * D), D)]
                        for a in parts:
                            last = mm(psum[:, FY, 0:D], act_part[:, a, f * P:(f + 1) * P], w,
                                      start=(n == 0), stop=(n == 3 * KF - 1))
                            n += 1
                last.then_inc(fy_mm, 1)

            def place_of(t):
                return pe.value_load(table[:, 1, bass.ds(t, 1)], min_val=0, max_val=(E - 1) * EW)

            def first_tile():
                pe.wait_ge(table_ready, 1)
                pe.wait_ge(piece_lo, E * PIECES)
                x_transposes(0, 0, 0, first=True)
                p = place_of(0)
                for m in range(NP):
                    hidden(0, p, m, first=True)
                x_transposes(1, 1, 0)

            def tile(t, s, nth, more, fresh):
                p = place_of(t)
                hidden(t, p, 0)
                act_transposes(t - 1, first=isinstance(t, int) and t == 1)
                hidden(t, p, 1)
                hidden(t, p, 2)
                if more:
                    s1 = (s + 1) % UN
                    x_transposes(t + 1, s1, nth + (1 if s1 == 0 else 0))
                down(t - 1, place_of(t - 1))

            def last_tile(t, s):
                act_transposes(t)
                down(t, place_of(t))

            ffn_tiles(pe, first_tile, tile, last_tile)

        @block.scalar
        def _(act):
            def ln_std(out_ap, var_ap):
                return nc.scalar.activation(out_ap, var_ap, ACT.Sqrt, bias=eps)

            def high(dst, src, scale):
                return nc.scalar.activation(dst, src, ACT.Copy, scale=scale)

            with nc.allow_non_contiguous_dma(reason="two short bias vectors and the gate"):
                for layer, b in enumerate((gnn_b1, gnn_b2)):
                    act.dma_start(bias[:, layer, :], b.rearrange("(k p) -> p k", p=P)).then_inc(small_in, 16)
                act.dma_start(wg_sb, wg.rearrange("(k p) e -> p k e", p=P)).then_inc(small_in, 16)
            for c in (2, 3):
                act.dma_start(x_all[:, TPC * c:TPC * (c + 1), :], x_t[:, TPC * c:TPC * (c + 1), :]
                              ).then_inc(x_arrived[c], 16)
            raw_w = gw_raw.rearrange("p (l k d) -> p l k d", l=2, k=2 * KD)
            for layer, w in enumerate((gnn_w1, gnn_w2)):
                act.dma_start(raw_w[:, layer, :, :], w.rearrange("(k p) d -> p k d", p=P)).then_inc(gw_in, 16)
            act.wait_ge(consts, 1)
            for c in range(NC):
                act.wait_ge(var_1, c + 1)
                ts = slice(TPC * c, TPC * (c + 1))
                ln_std(std_1[:, ts], mv_1[:, ts, 1]).then_inc(std_1_ready, 1)
            act.wait_ge(gw_in, 32)
            high(gwp[:, :, HI, :, :].rearrange("p l k d -> p l (k d)"),
                 gw_raw.rearrange("p (l k) -> p l k", l=2), S_W).then_inc(gw_hi, 1)
            for n in range(KD * NC):
                act.wait_ge(xt_tp, n + 1)
                high(acts(n // KD, HI, n % KD), psum[:, TP[n % 4], :],
                     S_ACT).then_inc(xt_hi, 1)

            def u_high(layer):
                for n in range(NT // 2):
                    act.wait_ge(u_mm, layer * (NT // 2) + n + 1)
                    high(u[:, HI, 2 * n:2 * n + 2, :].rearrange("p j d -> p (j d)"), psum[:, UB[n % 2], :],
                         S_ACT / S_SUM).then_inc(u_hi, 1)

            def block_high(c, g):
                r, jq = g // GPR, g % GPR
                act.wait_ge(adj_tp, c * GPC + (g + 1))
                high(adj_t[:, bass.ds(c, 1), HI, JB * jq:JB * (jq + 1), r * P:(r + 1) * P].rearrange(
                         "p a j w -> p (a j) w"),
                     psum[:, TP[g % 4], :].rearrange("p (j w) -> p j w", j=JB), S_W).then_inc(adj_hi, 1)

            def relu_1(c, f, first):
                if not first:
                    act.wait_ge(h_parts, KD * c + (f + 1 - KD))
                act.wait_ge(sum_mm, KD * c + (f + 1))
                nc.scalar.activation(sum_1[:, f, :], psum[:, SUM[f], :], ACT.Relu, scale=S_ACT / S_SUM,
                                     bias=bias_h[:, f:f + 1]).then_inc(sum_read, 1)

            u_high(0)
            for g in range(GPC):
                block_high(0, g)

            def layer_1(c, first, more):
                for f in range(KD):
                    if more:
                        for g in range(f * GPC // 2, (f + 1) * GPC // 2):
                            block_high(c + 1, g)
                    relu_1(c, f, first)

            act.wait_ge(bias_ready, 1)
            layer_1(0, True, True)
            with act.Fori(1, NC - 1) as c:
                layer_1(c, False, True)
            layer_1(NC - 1, False, False)
            u_high(1)

            def relu_2(c, f):
                act.wait_ge(sum_mm, KD * c + (KD * NC + f + 1))
                nc.scalar.activation(sum_2[:, f, :], psum[:, SUM[f], :], ACT.Relu, scale=1.0 / S_SUM,
                                     bias=bias[:, 1, f:f + 1]).then_inc(sum_read, 1)

            def load_x(c):
                act.dma_start(y_ch, x_t[:, bass.ds(c * TPC, TPC), :]).then_inc(x_again, 16)

            def piece_high(pair, m):
                act.wait_ge(piece_arrived[m % SLOTS], 32 * PIECES // SLOTS * pair + 16 * (m // SLOTS + 1))
                high(expert_piece(2 * pair + m // PIECES, m % PIECES, HI),
                     arriving[m % SLOTS].rearrange("p (a d) -> p a d", a=NP), S_W).then_inc(piece_hi, 1)

            def table_load(function):
                nc.scalar.activation(scratch, eps, function)

            def tail(c, pair, more, before_std, before_gate):
                table_load(ACT.Sqrt)
                for m in range(before_std):
                    piece_high(pair, m)
                act.wait_ge(var_2, c + 1)
                ln_std(std_2, mv_2[:, :, 1]).then_inc(std_2_ready, 1)
                act.wait_ge(y_ready, 2 * c + 2)
                act.dma_start(total_t[:, bass.ds(c * TPC, TPC), :], y_ch).then_inc(y_stored, 16)
                table_load(ACT.Exp)
                for m in range(before_std, before_gate):
                    piece_high(pair, m)
                for b in range(2):
                    act.wait_ge(xn2_tp, 2 * c + (b + 1))
                    nc.scalar.copy(xn2_t[:, b * CW:(b + 1) * CW], psum[:, XT[b], :]).then_inc(xn2_copied, 1)
                act.wait_ge(row_ready, 2 * c + 2)
                nc.scalar.copy(row[1][:, :, 0:D], row[0][:, :, 0:D]).then_inc(row_copied, 1)
                for m in range(before_gate, before_gate + 2):
                    piece_high(pair, m)
                if more:
                    act.wait_ge(y_stored, 16 * c + 16)
                    load_x(c + 1)
                    act.wait_ge(logits_mm, c + 1)
                    relu_2(c + 1, 0)
                act.wait_ge(gap_ready, c + 1)
                nc.scalar.activation(expd, gap, ACT.Exp).then_inc(exp_ready, 1)
                for m in range(before_gate + 2, 2 * PIECES):
                    piece_high(pair, m)
                if more:
                    relu_2(c + 1, 1)

            act.wait_ge(adj_tp, NC * GPC)
            load_x(0)
            for f in range(KD):
                relu_2(0, f)
            with act.Fori(0, NC - 1) as c:
                tail(c, c, True, 2, 5)
            act.wait_ge(o_ready, KD * NC)
            act.dma_start(b3_all[:, b3_early * F:], b3[b3_early:E, :].rearrange("e f -> (e f)").partition_broadcast(P)
                          ).then_inc(b3_arrived, 16)
            tail(NC - 1, NC - 1, False, 1, 3)
            table_load(ACT.Silu)

            def x_high(t):
                act.wait_ge(fx_tp, t + 1)
                high(x_part[:, HI, :], psum[:, FX, 0:D], S_ACT).then_inc(fx_hi, 1)

            def silu(t, first=False):
                act.wait_ge(hg_mm, t + 1)
                if not first:
                    act.wait_ge(act_ready, t)
                nc.scalar.activation(silu_h.rearrange("p (m w) -> p m w", m=NP), psum[:, 0:NP, 0:FP],
                                     ACT.Silu, scale=1.0 / S_SUM).then_inc(silu_ready, 1)

            def act_high(t):
                for b, (lo, hi) in enumerate(((0, CW), (CW, F))):
                    act.wait_ge(fa_tp, 2 * t + (b + 1))
                    high(act_part[:, HI, lo:hi], psum[:, FA[b], 0:hi - lo], 1.0).then_inc(fa_hi, 1)

            def first_tile():
                x_high(0)
                silu(0, first=True)
                x_high(1)

            def tile(t, s, nth, more, fresh):
                act_high(t - 1)
                silu(t)
                if more:
                    x_high(t + 1)

            ffn_tiles(act, first_tile, tile, lambda t, s: act_high(t))

        @block.vector
        def _(dve):
            step = Steps(dve, dve_step)
            v = nc.vector

            def low(dst, src, scale, hi_part):
                return v.scalar_tensor_tensor(out=dst, in0=src, scalar=scale, in1=hi_part,
                                              op0=ALU.mult, op1=ALU.subtract)

            def layernorm_stats(src, st, mv, n):
                for q in range(n):
                    ins = v.bn_stats(st[:, q, :], src[:, q, :])
                step.wait_for(ins)
                for q in range(n):
                    ins = v.bn_aggr(mv[:, q, :], st[:, q, :])
                return ins

            for c in range(NC):
                ts = slice(TPC * c, TPC * (c + 1))
                dve.wait_ge(x_arrived[c], 16)
                layernorm_stats(x_all[:, ts, :], st_1[:, ts, :], mv_1[:, ts, :], TPC).then_inc(var_1, 1)
            for c in range(NC):
                ts = slice(TPC * c, TPC * (c + 1))
                dve.wait_ge(std_1_ready, c + 1)
                step.wait_for(v.reciprocal(rstd_1[:, ts], std_1[:, ts]))
                for t in range(TPC * c, TPC * (c + 1)):
                    ins = v.tensor_scalar(xn_all[:, t, :], x_all[:, t, :], mv_1[:, t, 0:1], rstd_1[:, t:t + 1],
                                          ALU.subtract, ALU.mult)
                ins.then_inc(xn_ready, 1)
            dve.wait_ge(gw_hi, 1)
            low(gwp[:, :, LO, :, :].rearrange("p l k d -> p l (k d)"), gw_raw.rearrange("p (l k) -> p l k", l=2),
                S_W, gwp[:, :, HI, :, :].rearrange("p l k d -> p l (k d)")).then_inc(gw_lo, 1)
            dve.wait_ge(small_in, 48)
            v.tensor_scalar(bias_h, bias[:, 0, :], S_ACT, None, ALU.mult).then_inc(bias_ready, 1)
            for n in range(KD * NC):
                dve.wait_ge(xt_hi, n + 1)
                low(acts(n // KD, LO, n % KD), psum[:, TP[n % 4], :], S_ACT, acts(n // KD, HI, n % KD)
                    ).then_inc(xt_lo, 1)

            def u_low(layer):
                for n in range(NT // 2):
                    dve.wait_ge(u_hi, layer * (NT // 2) + n + 1)
                    low(u[:, LO, 2 * n:2 * n + 2, :].rearrange("p j d -> p (j d)"), psum[:, UB[n % 2], :],
                        S_ACT / S_SUM, u[:, HI, 2 * n:2 * n + 2, :].rearrange("p j d -> p (j d)")
                        ).then_inc(u_lo, 1)

            def block_low(c, g):
                r, jq = g // GPR, g % GPR
                dve.wait_ge(adj_hi, c * GPC + (g + 1))
                hi, lo = (adj_t[:, bass.ds(c, 1), h, JB * jq:JB * (jq + 1), r * P:(r + 1) * P].rearrange(
                    "p a j w -> p (a j) w") for h in (HI, LO))
                low(lo, psum[:, TP[g % 4], :].rearrange("p (j w) -> p j w", j=JB), S_W, hi).then_inc(adj_lo, 1)

            def h_split(c, f):
                dve.wait_ge(sum_read, KD * c + (f + 1))
                step.wait_for(v.tensor_copy(acts(c, HI, f), sum_1[:, f, :]))
                v.tensor_tensor(acts(c, LO, f), sum_1[:, f, :], acts(c, HI, f),
                                ALU.subtract).then_inc(h_parts, 1)

            u_low(0)
            for g in range(GPC):
                block_low(0, g)

            def layer_1(c, more):
                for f in range(KD):
                    if more:
                        for g in range(f * GPC // 2, (f + 1) * GPC // 2):
                            block_low(c + 1, g)
                    h_split(c, f)

            layer_1(0, True)
            base = step.n
            with dve.Fori(1, NC - 1) as c:
                step.base, step.n = base + (c - 1) * KD, 0
                layer_1(c, True)
            step.base, step.n = base + (NC - 2) * KD, 0
            layer_1(NC - 1, False)
            u_low(1)

            def add_h(c, f):
                dve.wait_ge(sum_read, KD * c + (KD * NC + f + 1))
                step.wait_for(v.scalar_tensor_tensor(
                    out=sum_2[:, f, :], in0=acts(c, LO, f), scalar=1.0 / S_ACT, in1=sum_2[:, f, :],
                    op0=ALU.mult, op1=ALU.add))
                v.scalar_tensor_tensor(
                    out=sum_2[:, f, :], in0=acts(c, HI, f), scalar=1.0 / S_ACT, in1=sum_2[:, f, :],
                    op0=ALU.mult, op1=ALU.add).then_inc(o_ready, 1)

            def piece_low(pair, m):
                dve.wait_ge(piece_hi, 2 * PIECES * pair + (m + 1))
                e, n = 2 * pair + m // PIECES, m % PIECES
                low(expert_piece(e, n, LO), arriving[m % SLOTS].rearrange("p (a d) -> p a d", a=NP), S_W,
                    expert_piece(e, n, HI)).then_inc(piece_lo, 1)

            def tail(c, pair, first, more, cuts):
                def pieces(i):
                    for m in range(([0] + cuts)[i], cuts[i]):
                        piece_low(pair, m)

                pieces(0)
                dve.wait_ge(x_again, 16 * c + 16)
                for b in range(2):
                    dve.wait_ge(o_tp, 2 * c + (b + 1))
                    y2 = y_ch[:, 2 * b:2 * b + 2, :].rearrange("p q d -> p (q d)")
                    v.scalar_tensor_tensor(out=y2, in0=psum[:, OT[b], :], scalar=0.0, in1=y2,
                                           op0=ALU.max, op1=ALU.add).then_inc(y_ready, 1)
                dve.wait_ge(y_ready, 2 * c + 2)
                layernorm_stats(y_ch, st_2, mv_2, TPC).then_inc(var_2, 1)
                pieces(1)
                dve.wait_ge(std_2_ready, c + 1)
                step.wait_for(v.reciprocal(rstd_2, std_2))
                if not first:
                    dve.wait_ge(scattered, c * (16 * TPC * TOP))
                for q in range(TPC):
                    ins = v.tensor_scalar(row[0][:, q, 0:D], y_ch[:, q, :], mv_2[:, q, 0:1], rstd_2[:, q:q + 1],
                                          ALU.subtract, ALU.mult)
                    if q % 2:
                        ins.then_inc(row_ready, 1)
                pieces(2)
                dve.wait_ge(logits_mm, c + 1)
                step.wait_for(v.tensor_copy(logits, psum[:, GATE, 0:TPC * E].rearrange("p (q e) -> p q e", q=TPC)))
                for q in range(TPC):
                    ins = v.max(best[:, q, :], logits[:, q, :])
                step.wait_for(ins)
                v.tensor_tensor(gap, best[:, :, 1], best[:, :, 0], ALU.subtract).then_inc(gap_ready, 1)
                for q in range(TPC):
                    ins = v.max_index(best_ix[:, q, :], best[:, q, :], logits[:, q, :])
                step.wait_for(ins)
                step.wait_for(v.tensor_copy(choice, best_ix[:, :, 0:TOP]))
                pick = small["choice"].unsqueeze(2).to_broadcast([P, TPC * TOP, E])
                step.wait_for(v.tensor_tensor(
                    small["onehot"].rearrange("p (i e) -> p i e", e=E), pick,
                    iota_e.unsqueeze(1).to_broadcast([P, TPC * TOP, E]), ALU.is_equal))
                v.tensor_tensor(mask, onehot[:, :, 0, :], onehot[:, :, 1, :], ALU.add).then_inc(mask_ready, 1)
                pieces(3)
                dve.wait_ge(exp_ready, c + 1)
                step.wait_for(v.tensor_scalar(den, expd, 1.0, None, ALU.add))
                step.wait_for(v.reciprocal(row[0][:, :, D], den))
                v.tensor_tensor(row[1][:, :, D], expd, row[0][:, :, D], ALU.mult).then_inc(weights_ready, 1)
                dve.wait_ge(rank_mm, c + 1)
                v.tensor_tensor(place, psum[:, GATE, 64:64 + TPC * E].rearrange("p (q e) -> p q e", q=TPC),
                                region_0.unsqueeze(1).to_broadcast([P, TPC, E]), ALU.add).then_inc(gate_read, 1)
                with nc.allow_low_precision(reason="counts up to 16"):
                    step.wait_for(v.tensor_reduce(added, mask.rearrange("p q e -> p e q"), AX_X, ALU.add))
                v.tensor_tensor(carry, carry, added, ALU.add).then_inc(carried, 1)
                dve.wait_ge(gate_read, c + 1)
                for k in range(TOP):
                    ins = v.tensor_tensor(picked[:, :, k, :], onehot[:, :, k, :], place, ALU.mult)
                step.wait_for(ins)
                step.wait_for(v.tensor_reduce(slot_f, small["picked"].rearrange("p (i e) -> p i e", e=E),
                                              AX_X, ALU.add))
                v.tensor_copy(slot, slot_f).then_inc(slots_ready, 1)
                if more:
                    pieces(4)
                    add_h(c + 1, 0)
                    pieces(5)
                    add_h(c + 1, 1)

            for f in range(KD):
                add_h(0, f)
            for c in range(NC):
                tail(c, c, c == 0, c < NC - 1, [2, 3, 7, 8, 10, 12] if c < NC - 1 else [1, 2, 5, 5])

            dve.wait_ge(late_consts, 1)
            dve.wait_ge(count_mm, 1)
            step.wait_for(v.tensor_copy(n_e, psum[0:1, COUNT, 0:E]))
            step.wait_for(v.tensor_tensor(pad_f, n_e, region_0[0:1, :], ALU.add))
            v.tensor_copy(pad_row, pad_f).then_inc(pads_known, 1)
            for m in range(5, 8):
                piece_low(NC - 1, m)
            step.wait_for(v.tensor_tensor(over_k, n_e.unsqueeze(2).to_broadcast([1, E, NT]),
                                          iota_k.unsqueeze(1).to_broadcast([1, E, NT]), ALU.is_gt))
            step.wait_for(v.tensor_reduce(nt_e, over_k, AX_X, ALU.add))
            v.memset(delta[:, 0:1], 0.0)
            v.tensor_scalar(delta[:, 1:E], nt_e[:, 0:E - 1], -float(P), float(REG), ALU.mult, ALU.add)
            step.wait_for(v.tensor_tensor(over_e, nt_e.unsqueeze(1).to_broadcast([1, E, E]), upto, ALU.mult))
            step.wait_for(v.tensor_reduce(last, over_e, AX_X, ALU.add))
            step.wait_for(v.tensor_tensor(first, last, nt_e, ALU.subtract))
            step.wait_for(v.tensor_tensor(started, iota_n.unsqueeze(2).to_broadcast([1, TILES, E]),
                                          first.unsqueeze(1).to_broadcast([1, TILES, E]), ALU.is_ge))
            v.tensor_reduce(experts_seen, started, AX_X, ALU.add)
            step.wait_for(v.tensor_tensor(shifts, started, delta.unsqueeze(1).to_broadcast([1, TILES, E]), ALU.mult))
            step.wait_for(v.tensor_reduce(row_shift, shifts, AX_X, ALU.add))
            step.wait_for(v.scalar_tensor_tensor(out=tab_f[:, 0, :], in0=iota_n, scalar=float(P), in1=row_shift,
                                                 op0=ALU.mult, op1=ALU.add))
            v.tensor_scalar(tab_f[:, 0, :], tab_f[:, 0, :], pad_f[:, E - 1:E], None, ALU.min)
            v.tensor_scalar(tab_f[:, 1, :], experts_seen, float(EW), -float(EW), ALU.mult, ALU.add)
            step.wait_for(v.tensor_scalar(tab_f[:, 2, :], experts_seen, float(F), -float(F), ALU.mult, ALU.add))
            v.tensor_copy(table, tab_f).then_inc(table_ready, 1)
            for m in range(8, 2 * PIECES):
                piece_low(NC - 1, m)

            def token_copy(t, s, nth, fresh):
                dve.wait_ge(xin_arrived[s], 16 * nth + 16)
                if not fresh:
                    dve.wait_ge(fy_added, 16 * t + 16 * (1 - UN))
                v.tensor_copy(token_w[:, s:s + 1], x_in[:, s, D:D + 1])
                v.tensor_copy(token_ix[:, s:s + 1], x_in[:, s, D + 1:D + 2]).then_inc(token_read, 1)

            def x_low(t):
                dve.wait_ge(fx_hi, t + 1)
                low(x_part[:, LO, :], psum[:, FX, 0:D], S_ACT, x_part[:, HI, :]).then_inc(fx_lo, 1)

            def gate_g(t, first=False):
                b = dve.value_load(table[:, 2, bass.ds(t, 1)], min_val=0, max_val=(E - 1) * F)
                dve.wait_ge(silu_ready, t + 1)
                v.scalar_tensor_tensor(out=gated.rearrange("p (m w) -> p m w", m=NP), in0=psum[:, 0:NP, FP:2 * FP],
                                       scalar=1.0 / S_SUM, in1=b3_all[:, bass.ds(b, F)].rearrange(
                                           "p (m w) -> p m w", m=NP), op0=ALU.mult, op1=ALU.add
                                       ).then_inc(gated_ready, 1)

            def activate(t, first=False):
                dve.wait_ge(gated_ready, t + 1)
                if not first:
                    dve.wait_ge(fa_tp, 2 * t)
                v.scalar_tensor_tensor(out=act_f, in0=gated, scalar=S_ACT, in1=silu_h,
                                       op0=ALU.mult, op1=ALU.mult).then_inc(act_ready, 1)

            def act_low(t):
                for b, (lo, hi) in enumerate(((0, CW), (CW, F))):
                    dve.wait_ge(fa_hi, 2 * t + (b + 1))
                    v.tensor_tensor(act_part[:, LO, lo:hi], psum[:, FA[b], 0:hi - lo], act_part[:, HI, lo:hi],
                                    ALU.subtract).then_inc(fa_lo, 1)

            def y_weigh(t, s):
                dve.wait_ge(fy_mm, t + 1)
                dve.wait_ge(token_read, t + 1)
                v.tensor_scalar(y_out[:, s, :], psum[:, FY, 0:D], token_w[:, s:s + 1], 1.0 / S_SUM,
                                ALU.mult, ALU.mult).then_inc(fy_ready, 1)

            def first_tile():
                dve.wait_ge(b3_early_in, 16)
                dve.wait_ge(b3_arrived, 16)
                dve.wait_ge(table_ready, 1)
                x_low(0)
                token_copy(0, 0, 0, fresh=True)
                gate_g(0)
                x_low(1)
                activate(0, first=True)

            def tile(t, s, nth, more, fresh):
                act_low(t - 1)
                token_copy(t, s, nth, fresh)
                gate_g(t)
                if more:
                    x_low(t + 1)
                activate(t)
                y_weigh(t - 1, (s - 1) % UN)

            def last_tile(t, s):
                act_low(t)
                y_weigh(t, s)

            ffn_tiles(dve, first_tile, tile, last_tile)


_INS = ['x', 'adj', 'L0_gnn_W1', 'L0_gnn_b1', 'L0_gnn_W2', 'L0_gnn_b2', 'L0_ffn_Wg', 'L0_ffn_W1',
        'L0_ffn_W2', 'L0_ffn_W3', 'L0_ffn_b3']
_OUTS = [((2048, 256), 'float32')]


def kernel(**inputs):
    import numpy as _np
    import concourse.bacc as _bacc
    from concourse import mybir as _mybir
    from concourse.bass_utils import run_bass_kernel_spmd as _run

    nc = _bacc.Bacc("TRN2", target_bir_lowering=False, num_devices=1)
    arrays, args = {}, []
    for name in _INS:
        a = _np.ascontiguousarray(inputs[name])
        arrays[f"in_{name}_dram"] = a
        args.append(nc.dram_tensor(f"in_{name}_dram", a.shape, _mybir.dt.from_np(a.dtype), kind="ExternalInput").ap())
    for i, (shape, dtype) in enumerate(_OUTS):
        dt = _mybir.dt.from_np(_np.dtype(dtype))
        args.append(nc.dram_tensor(f"out_{i}_dram", shape, dt, kind="ExternalOutput").ap())
    moe_gnn_kernel(nc, *args)
    r = _run(nc, [arrays], core_ids=[0])
    got = tuple(r.results[0][f"out_{i}_dram"] for i in range(len(_OUTS)))
    return got[0]
```

```python
from contextlib import ExitStack

import concourse.bass as bass
from concourse import mybir

P = 128
F32, F16 = mybir.dt.float32, mybir.dt.float16
I32, U32 = mybir.dt.int32, mybir.dt.uint32
ALU = mybir.AluOpType
ACT = mybir.ActivationFunctionType
AX_X = mybir.AxisListType.X

S_ACT = 16.0
S_W = 1024.0
S_SUM = S_ACT * S_W
EPS = 1e-5
HI, LO = 0, 1
PASSES = ((HI, HI), (LO, HI), (HI, LO))
TOP = 2


class Steps:

    def __init__(self, eng, sem):
        self.eng, self.sem, self.base, self.n = eng, sem, 0, 0

    def wait_for(self, ins):
        self.n += 1
        ins.then_inc(self.sem, 1)
        self.eng.wait_ge(self.sem, self.base + self.n)


def moe_gnn_kernel(nc, x, adj, gnn_w1, gnn_b1, gnn_w2, gnn_b2, wg, w1, w2, w3, b3, out):
    N, D = x.shape
    E, _, F = w1.shape
    NT, KD, KF = N // P, D // P, F // P
    CW = 512
    NC, TPC = N // CW, CW // P
    JB = CW // P
    GPC = TPC * NT // JB
    GPR = GPC // TPC
    NP = 3
    FP = F // NP
    ROW = D + 2
    REG = N + P
    TILES = TOP * N // P + E - 1
    UN = 3
    W13 = 2 * KD * NP * CW
    EW = W13 + 2 * KF * D
    ADJC = 2 * NT * CW
    EXT = E * EW - NC * ADJC
    PIECES = 2 * KD + 2
    SLOTS = 3
    assert 2 * FP == CW and NC == 4 and TPC == 4 and EXT == 4 * N and EW <= ADJC
    assert TILES % UN == 0 and KF == 2 * NP and GPC == NT and E == 2 * NC
    assert PIECES % SLOTS == 0

    routed = nc.dram_tensor("routed_rows", (E * REG, ROW), F32, kind="Internal").ap()
    total = nc.dram_tensor("row_sums", (N + P, D), F32, kind="Internal").ap()
    x_t = x.rearrange("(t p) d -> p t d", p=P)
    total_t = total.rearrange("(t p) d -> p t d", p=P)

    with ExitStack() as ctx:
        def sb(name, shape, dt):
            return ctx.enter_context(nc.sbuf_tensor(name, shape, dt))

        def sem(name):
            return ctx.enter_context(nc.semaphore(name))

        big = sb("big", [P, E * EW], F16)
        tu = sb("tu", [P, 2 * KD * N + 2 * NT * D], F16)
        rb = sb("rb", [P, 2 * N], F32)
        gw = sb("gw", [P, 2 * 2 * 2 * KD * D], F16)
        stage = sb("stage", [P, 2, F], F32)
        ident = sb("ident", [P, P], F32)
        before = sb("before", [P, P], F16)
        ones = sb("ones", [P, P], F16)
        fixed = sb("fixed", [P, 76], F32)
        bias = fixed[:, 0:4].rearrange("p (l k) -> p l k", l=2)
        bias_h = fixed[:, 4:6]
        wg_sb = fixed[:, 6:6 + KD * E].rearrange("p (k e) -> p k e", k=KD)
        eps = fixed[:, 22:23]
        scratch = fixed[:, 23:24]
        iota_e = fixed[:, 24:32]
        region_0 = fixed[:, 32:40]
        token_no = fixed[:, 40:56]
        token_w = fixed[:, 56:56 + UN]
        token_ix = fixed[:, 60:60 + UN].bitcast(U32)
        rstd_2 = fixed[:, 64:68]
        std_2 = fixed[:, 68:72]
        carry = fixed[:, 72:76].bitcast(F16)

        adj_t = big[:, EXT:].rearrange("p (c h j w) -> p c h j w", c=NC, h=2, j=NT)
        low_rows = big[:, 0:EXT].bitcast(F32)
        adj_rows = [low_rows[:, 0:N], low_rows[:, N:2 * N], rb[:, 0:N], rb[:, N:2 * N]]
        late = EXT + (NC - 1) * ADJC
        x_all = big[:, late:late + ADJC // 2].bitcast(F32).rearrange("p (t d) -> p t d", t=NT)
        xn_all = big[:, late + ADJC // 2:].bitcast(F32).rearrange("p (t d) -> p t d", t=NT)
        raw = big[:, late - ADJC:late].bitcast(F32)
        gw_raw = raw[:, 0:4 * KD * D]
        st_1 = raw[:, 4 * KD * D:4 * KD * D + 6 * NT].rearrange("p (t s) -> p t s", t=NT)
        mv_1 = raw[:, 4 * KD * D + 128:4 * KD * D + 128 + 2 * NT].rearrange("p (t s) -> p t s", t=NT)
        std_1 = raw[:, 4 * KD * D + 160:4 * KD * D + 160 + NT]
        rstd_1 = raw[:, 4 * KD * D + 176:4 * KD * D + 176 + NT]
        shift_1 = raw[:, 4 * KD * D + 192:4 * KD * D + 192 + NT]
        act_t = tu[:, 0:2 * KD * N].rearrange("p (c h k w) -> p c h k w", c=NC, h=2, k=KD)
        u = tu[:, 2 * KD * N:].rearrange("p (h j d) -> p h j d", h=2, j=NT)
        gwp = gw[:, :].rearrange("p (l h k d) -> p l h k d", l=2, h=2, k=2 * KD)
        sum_1 = stage[:, :, 0:CW]
        arriving = [stage[:, 0, :], stage[:, 1, :], tu[:, 0:2 * F].bitcast(F32)]
        sum_2 = gw[:, 0:2 * 2 * KD * D].bitcast(F32).rearrange("p (f w) -> p f w", f=KD)
        xn2_t = gw[:, 0:2 * 2 * KD * D].bitcast(F32)

        y_ch = rb[:, 0:TPC * D].rearrange("p (q d) -> p q d", q=TPC)
        at = TPC * D
        row = []
        for k in range(TOP):
            row.append(rb[:, at:at + TPC * ROW].rearrange("p (q d) -> p q d", q=TPC))
            at += TPC * ROW
        small = {}
        for name, n in (("st_2", 24), ("mv_2", 8), ("logits", 32), ("best", 32), ("best_ix", 32),
                        ("choice", 8), ("onehot", 64), ("place", 32), ("picked", 64),
                        ("slot_f", 8), ("slot", 8), ("gap", 4), ("expd", 4), ("den", 4),
                        ("mask", 16), ("added", 4)):
            small[name] = rb[:, at:at + n]
            at += n
        st_2 = small["st_2"].rearrange("p (q s) -> p q s", q=TPC)
        mv_2 = small["mv_2"].rearrange("p (q s) -> p q s", q=TPC)
        logits = small["logits"].rearrange("p (q e) -> p q e", q=TPC)
        best = small["best"].rearrange("p (q e) -> p q e", q=TPC)
        best_ix = small["best_ix"].bitcast(U32).rearrange("p (q e) -> p q e", q=TPC)
        choice = small["choice"].rearrange("p (q k) -> p q k", q=TPC)
        onehot = small["onehot"].rearrange("p (q k e) -> p q k e", q=TPC, k=TOP)
        picked = small["picked"].rearrange("p (q k e) -> p q k e", q=TPC, k=TOP)
        place = small["place"].rearrange("p (q e) -> p q e", q=TPC)
        slot_f, slot = small["slot_f"], small["slot"].bitcast(U32)
        gap, expd, den = small["gap"], small["expd"], small["den"]
        mask = small["mask"].bitcast(F16).rearrange("p (q e) -> p q e", q=TPC)
        added = small["added"].bitcast(F16)
        iota_k = rb[0:1, at:at + NT]
        upto = rb[0:1, at + 16:at + 80].rearrange("p (a b) -> p a b", a=E)
        iota_n = rb[0:1, at + 80:at + 80 + TILES]
        cnt = rb[0:1, at + 120:at + 120 + 8 * E]
        n_e, nt_e, last, first, delta, pad_f = (cnt[:, E * i:E * i + E] for i in range(6))
        pad_row = cnt[:, 6 * E:7 * E].bitcast(I32)
        experts_seen = rb[0:1, at + 184:at + 184 + TILES]
        row_shift = rb[0:1, at + 224:at + 224 + TILES]
        tab_f = rb[0:1, at + 264:at + 264 + 3 * TILES].rearrange("p (a t) -> p a t", a=3)
        assert at + 264 + 3 * TILES <= 2 * N
        wide = gw[0:1, 0:4 * KD * D].bitcast(F32)
        over_k = wide[:, 0:E * NT].rearrange("p (e k) -> p e k", e=E)
        over_e = wide[:, 128:128 + E * E].rearrange("p (a b) -> p a b", a=E)
        started = wide[:, 192:192 + E * TILES].rearrange("p (t e) -> p t e", e=E)
        shifts = wide[:, 512:512 + E * TILES].rearrange("p (t e) -> p t e", e=E)
        gw_2 = gw[:, 4 * KD * D:]
        x_in = gw_2[:, 0:2 * UN * ROW].bitcast(F32).rearrange("p (s d) -> p s d", s=UN)
        table = gw_2[0:1, 2 * UN * ROW:2 * UN * ROW + 6 * TILES].bitcast(I32).rearrange(
            "p (a t) -> p a t", a=3)

        b3_all = tu[:, 2 * F:2 * F + 2 * E * F].bitcast(F32)
        free = 2 * F + 2 * E * F
        b3_early = ((NC - 1) * 2 * KD * CW - 2 * F) // (2 * F)
        pad = tu[:, free:free + 2 * ROW].bitcast(F32)
        free += 2 * ROW
        x_part = tu[:, free:free + 2 * D].rearrange("p (h d) -> p h d", h=2)
        silu_h, gated, act_f = (rb[:, F * i:F * i + F] for i in range(3))
        act_part = rb[:, 3 * F:4 * F].bitcast(F16).rearrange("p (h f) -> p h f", h=2)
        y_out = rb[:, 4 * F:4 * F + UN * D].rearrange("p (s d) -> p s d", s=UN)

        psum = ctx.enter_context(nc.psum_tensor("psum", [P, 8, CW], F32))
        SUM = (0, 1)
        TP = (2, 3, 4, 5)
        UB = (6, 7)
        OT, XT, GATE, COUNT = (2, 3), (4, 5), 6, 7
        FA, FX, FY = (3, 4), 5, 6
        HG = ((0, NP - 1), (NP - 1, NP))

        small_in = sem("small_in")
        gw_arrived = [sem(f"gw_arrived{layer}") for layer in range(2)]
        x_arrived = [sem(f"x_arrived{c}") for c in range(NC)]
        row_arrived = [sem(f"row_arrived{r}") for r in range(TPC)]
        piece_arrived = [sem(f"piece_arrived{s}") for s in range(SLOTS)]
        xin_arrived = [sem(f"xin_arrived{s}") for s in range(UN)]
        consts, zeroed, late_consts = sem("consts"), sem("zeroed"), sem("late_consts")
        dve_step, pool_step = sem("dve_step"), sem("pool_step")
        var_1, std_1_ready, xn_act, bias_ready = sem("var_1"), sem("std_1_ready"), sem("xn_act"), sem("bias_ready")
        xn_dve = sem("xn_dve")
        gw_ready, scaled_1 = sem("gw_ready"), sem("scaled_1")
        xt_tp, xt_hi, xt_lo = sem("xt_tp"), sem("xt_hi"), sem("xt_lo")
        u_mm, u_hi, u_lo = sem("u_mm"), sem("u_hi"), sem("u_lo")
        adj_tp, adj_hi, adj_lo = sem("adj_tp"), sem("adj_hi"), sem("adj_lo")
        sum_mm, sum_read, h_parts, o_ready = sem("sum_mm"), sem("sum_read"), sem("h_parts"), sem("o_ready")
        o_tp, x_again, y_ready, y_stored = sem("o_tp"), sem("x_again"), sem("y_ready"), sem("y_stored")
        var_2, std_2_ready, row_ready = sem("var_2"), sem("std_2_ready"), sem("row_ready")
        row_copied = sem("row_copied")
        xn2_tp, xn2_copied, logits_mm = sem("xn2_tp"), sem("xn2_copied"), sem("logits_mm")
        gap_ready, exp_ready, mask_ready, rank_mm = sem("gap_ready"), sem("exp_ready"), sem("mask_ready"), sem("rank_mm")
        gate_read, slots_ready, weights_ready = sem("gate_read"), sem("slots_ready"), sem("weights_ready")
        scattered, carried = sem("scattered"), sem("carried")
        piece_hi, piece_lo = sem("piece_hi"), sem("piece_lo")
        count_mm, pads_known, table_ready = sem("count_mm"), sem("pads_known"), sem("table_ready")
        pad_built, pad_stored, b3_arrived = sem("pad_built"), sem("pad_stored"), sem("b3_arrived")
        b3_early_in = sem("b3_early_in")
        token_read = sem("token_read")
        fx_tp, fx_hi, fx_lo = sem("fx_tp"), sem("fx_hi"), sem("fx_lo")
        hg_mm, silu_ready, gated_ready, act_ready = sem("hg_mm"), sem("silu_ready"), sem("gated_ready"), sem("act_ready")
        fa_tp, fa_hi, fa_lo = sem("fa_tp"), sem("fa_hi"), sem("fa_lo")
        fy_mm, fy_ready, fy_added, out_stored = sem("fy_mm"), sem("fy_ready"), sem("fy_added"), sem("out_stored")

        def ffn_tiles(eng, first_tile, tile, last_tile):
            first_tile()
            for t in range(1, UN):
                tile(t, t, 0, True, True)
            with eng.Fori(1, TILES // UN - 1) as i:
                for s in range(UN):
                    tile(i * UN + s, s, i, True, False)
            for t in range(TILES - UN, TILES):
                tile(t, t % UN, t // UN, t < TILES - 1, False)
            last_tile(TILES - 1, (TILES - 1) % UN)

        def expert_piece(e, n, part):
            mine = big[:, bass.ds(e * EW, EW)]
            if n < 2 * KD:
                v = mine[:, 0:W13].rearrange("p (k h m w) -> p k h m w", k=KD, h=2, m=NP)
                side = n // KD
                return v[:, n % KD, part, :, side * FP:(side + 1) * FP]
            v = mine[:, W13:].rearrange("p (f h d) -> p f h d", f=KF, h=2)
            half = n - 2 * KD
            return v[:, NP * half:NP * (half + 1), part, :]

        def acts(c, part, k):
            return act_t[:, bass.ds(c, 1), part, k, :].rearrange("p a w -> p (a w)")

        def load_piece(eng, e, n):
            if n < 2 * KD:
                w, k = (w1, w3)[n // KD], n % KD
                src = w[bass.ds(e, 1), k * P:(k + 1) * P, :].rearrange("a p f -> (a p) f")
                dst = arriving[n % SLOTS]
            else:
                h = n - 2 * KD
                src = w2[bass.ds(e, 1), h * NP * P:(h + 1) * NP * P, :].rearrange(
                    "a (f p) d -> (a p) f d", p=P)
                dst = arriving[n % SLOTS].rearrange("p (f d) -> p f d", f=NP)
            eng.dma_start(dst, src).then_inc(piece_arrived[n % SLOTS], 16)

        def load_last(eng, n):
            eng.wait_ge(piece_lo, (E - 1) * PIECES + (n + 1 - SLOTS))
            load_piece(eng, E - 1, n)

        def store_pad(eng, e):
            end = eng.value_load(pad_row[:, e:e + 1], min_val=e * REG, max_val=e * REG + N)
            eng.dma_start(routed[bass.ds(end, P), :], pad[:, :]).then_inc(pad_stored, 16)

        AHEAD = NT // 2 - 4

        def block_of(g, first):
            return (g % TPC, g // TPC) if first else (g // GPR, g % GPR)

        def start_order(normalize, transposed, times_w, block_0):
            normalize(0)
            normalize(1)
            transposed(0)
            normalize(2)
            transposed(1)
            times_w(0)
            times_w(1)
            normalize(3)
            transposed(2)
            times_w(2)
            times_w(3)
            transposed(3)
            for n in range(4, NT // 2):
                times_w(n)
                block_0(n - 4)

        block = ctx.enter_context(nc.Block())

        @block.sync
        def _(sp):
            for c in range(NC):
                sp.dma_start(x_all[:, TPC * c:TPC * (c + 1), :], x_t[:, TPC * c:TPC * (c + 1), :]
                             ).then_inc(x_arrived[c], 16)
            for r in range(TPC):
                sp.dma_start(adj_rows[r], adj[r * P:(r + 1) * P, :]).then_inc(row_arrived[r], 16)
            for r in range(TPC):
                sp.wait_ge(adj_tp, GPC - TPC + (r + 1))
                sp.dma_start(adj_rows[r], adj[(TPC + r) * P:(TPC + r + 1) * P, :]).then_inc(row_arrived[r], 16)
            with sp.Fori(2, NC) as c:
                for r in range(TPC):
                    sp.wait_ge(adj_tp, (c - 1) * GPC + (r + 1) * GPR)
                    sp.dma_start(adj_rows[r], adj[bass.ds((c * TPC + r) * P, P), :]
                                 ).then_inc(row_arrived[r], 16)

            sp.wait_ge(h_parts, KD * NC)
            for n in range(PIECES):
                if n == SLOTS - 1:
                    sp.wait_ge(o_ready, KD)
                if n >= SLOTS:
                    sp.wait_ge(piece_lo, n + 1 - SLOTS)
                load_piece(sp, 0, n)
            with sp.Fori(1, E - 1) as e:
                for n in range(PIECES):
                    sp.wait_ge(piece_lo, e * PIECES + (n + 1 - SLOTS))
                    load_piece(sp, e, n)

            for n in range(SLOTS):
                load_last(sp, n)
            sp.wait_ge(pad_built, 1)
            sp.dma_start(total[N:N + P, :], pad[:, 0:D]).then_inc(pad_stored, 16)
            sp.wait_ge(pads_known, 1)
            for e in range(E - 2):
                store_pad(sp, e)
            sp.wait_ge(pad_stored, 16 * (E + 1))
            sp.wait_ge(scattered, 16 * NT * TOP)
            sp.wait_ge(y_stored, 16 * NC)
            sp.wait_ge(table_ready, 1)

            def load_tile(t, s):
                start = sp.value_load(table[:, 0, bass.ds(t, 1)], min_val=0, max_val=E * REG - P)
                sp.dma_start(x_in[:, s, :], routed[bass.ds(start, P), :]).then_inc(xin_arrived[s], 16)

            for t in range(UN):
                load_tile(t, t)
            with sp.Fori(1, TILES // UN) as i:
                for s in range(UN):
                    sp.wait_ge(fx_tp, (i - 1) * UN + (s + 1))
                    sp.wait_ge(token_read, (i - 1) * UN + (s + 1))
                    load_tile(i * UN + s, s)
            sp.wait_ge(fy_added, 16 * TILES)
            sp.dma_start(out, total[0:N, :]).then_inc(out_stored, 16)
            sp.wait_ge(out_stored, 16)

        @block.gpsimd
        def _(pool):
            step = Steps(pool, pool_step)
            nc.gpsimd.memset(ident[:], 0.0)
            nc.gpsimd.memset(ones[:], 1.0)
            nc.gpsimd.memset(carry, 0.0)
            nc.gpsimd.memset(eps, EPS)
            nc.gpsimd.iota(iota_e, pattern=[[1, E]], base=0, channel_multiplier=0,
                           allow_small_or_imprecise_dtypes=True)
            nc.gpsimd.iota(region_0, pattern=[[REG, E]], base=0, channel_multiplier=0,
                           allow_small_or_imprecise_dtypes=True)
            step.wait_for(nc.gpsimd.iota(token_no, pattern=[[P, NT]], base=0, channel_multiplier=1,
                                         allow_small_or_imprecise_dtypes=True))
            nc.gpsimd.affine_select(out=before[:], in_=ones[:], compare_op=ALU.is_gt, fill=0.0,
                                    base=0, pattern=[[1, P]], channel_multiplier=-1)
            nc.gpsimd.affine_select(out=ident[:], in_=ident[:], compare_op=ALU.not_equal, fill=1.0,
                                    base=0, pattern=[[-1, P]], channel_multiplier=1
                                    ).then_inc(consts, 1)
            raw_parts = gw_raw.rearrange("p (l k d) -> p l k d", l=2, k=2 * KD)
            for layer, k0, k1 in ((0, KD, 2 * KD), (0, 0, KD), (1, 0, 2 * KD)):
                if k0 != 0 or layer:
                    pool.wait_ge(gw_arrived[layer], 16)
                src = raw_parts[:, layer, k0:k1, :]
                hi, lo = (gwp[:, layer, part, k0:k1, :] for part in (HI, LO))
                step.wait_for(nc.gpsimd.tensor_scalar(src, src, S_W, None, ALU.mult))
                step.wait_for(nc.gpsimd.tensor_copy(hi, src))
                nc.gpsimd.tensor_tensor(lo, src, hi, ALU.subtract).then_inc(gw_ready, 1)
            pool.wait_ge(adj_tp, NC * GPC)
            nc.gpsimd.iota(iota_k, pattern=[[P, NT]], base=0, channel_multiplier=0,
                           allow_small_or_imprecise_dtypes=True)
            nc.gpsimd.iota(iota_n, pattern=[[1, TILES]], base=0, channel_multiplier=0,
                           allow_small_or_imprecise_dtypes=True)
            step.wait_for(nc.gpsimd.memset(upto, 1.0))
            nc.gpsimd.affine_select(out=upto, in_=upto, compare_op=ALU.is_ge, fill=0.0, base=0,
                                    pattern=[[1, E], [-1, E]], channel_multiplier=0
                                    ).then_inc(late_consts, 1)

            def scatter(c, first):
                if not first:
                    pool.wait_ge(scattered, c * (16 * TPC * TOP))
                for k in range(TOP):
                    ins = nc.gpsimd.tensor_copy(row[k][:, :, D + 1], token_no[:, bass.ds(c * TPC, TPC)])
                step.wait_for(ins)
                pool.wait_ge(row_copied, c + 1)
                pool.wait_ge(slots_ready, c + 1)
                pool.wait_ge(weights_ready, c + 1)
                for q in range(TPC):
                    for k in range(TOP):
                        i = q * TOP + k
                        nc.gpsimd.indirect_dma_start(
                            out=routed, out_offset=bass.IndirectOffsetOnAxis(ap=slot[:, i:i + 1], axis=0),
                            in_=row[k][:, q, :], in_offset=None).then_inc(scattered, 16)

            for c in range(NC - 1):
                scatter(c, c == 0)

            pool.wait_ge(o_ready, KD * (NC - 1))
            pool.dma_start(b3_all[:, 0:b3_early * F], b3[0:b3_early, :].rearrange("e f -> (e f)").partition_broadcast(P)
                           ).then_inc(b3_early_in, 16)

            pool.wait_ge(sum_mm, 2 * KD * NC)
            nc.gpsimd.iota(pad[:, D + 1:D + 2], pattern=[[0, 1]], base=N, channel_multiplier=1,
                           allow_small_or_imprecise_dtypes=True)
            nc.gpsimd.memset(pad[:, 0:D + 1], 0.0).then_inc(pad_built, 1)

            scatter(NC - 1, False)

            pool.wait_ge(y_stored, 16 * NC)
            pool.wait_ge(pad_stored, 16)
            for t in range(TILES):
                pool.wait_ge(fy_ready, t + 1)
                if t:
                    pool.wait_ge(fy_added, 16 * t)
                s = t % UN
                nc.gpsimd.indirect_dma_start(
                    out=total, out_offset=bass.IndirectOffsetOnAxis(ap=token_ix[:, s:s + 1], axis=0),
                    in_=y_out[:, s, :], in_offset=None, compute_op=ALU.add).then_inc(fy_added, 16)

        @block.tensor
        def _(pe):
            mm = nc.tensor.matmul
            pe.wait_ge(consts, 1)

            def x_chunk(c):
                pe.wait_ge(xn_dve, c + 1)
                pe.wait_ge(xn_act, c + 1)
                for k in range(KD):
                    n = KD * c + k
                    if n >= len(TP):
                        pe.wait_ge(xt_lo, n - len(TP) + 1)
                    for q in range(TPC):
                        last = nc.tensor.transpose(psum[:, TP[n % 4], q * P:(q + 1) * P],
                                                   xn_all[:, TPC * c + q, k * P:(k + 1) * P], ident[:])
                    last.then_inc(xt_tp, 1)

            def rows_times_w(layer, n):
                if layer == 0:
                    pe.wait_ge(xt_lo, KD * (n // 2 + 1))
                else:
                    pe.wait_ge(h_parts, KD * (n // 2 + 1))
                if n == 0:
                    pe.wait_ge(gw_ready, 1 if layer == 0 else 3)
                if layer or n >= 2:
                    pe.wait_ge(u_lo, layer * (NT // 2) + n - 1)
                for j in range(2):
                    jt = 2 * n + j
                    for i, (k, (a, b)) in enumerate((k, ab) for k in range(KD) for ab in PASSES):
                        last = mm(psum[:, UB[n % 2], j * D:(j + 1) * D],
                                  acts(jt // TPC, a, k)[:, (jt % TPC) * P:(jt % TPC + 1) * P], gwp[:, layer, b, KD + k, :],
                                  start=(i == 0), stop=(i == 3 * KD - 1))
                last.then_inc(u_mm, 1)

            def transpose_group(c, g, first):
                r, jq = block_of(g, first)
                if jq == 0:
                    pe.wait_ge(row_arrived[r], 16 * c + 16)
                if first and g < 4:
                    pe.wait_ge(xt_lo, KD * NC - 4 + g + 1)
                else:
                    pe.wait_ge(adj_lo, c * GPC + (g - 3))
                for b in range(JB):
                    j = JB * jq + b
                    last = nc.tensor.transpose(psum[:, TP[g % 4], b * P:(b + 1) * P],
                                               adj_rows[r][:, j * P:(j + 1) * P], ident[:])
                last.then_inc(adj_tp, 1)

            def chunk(layer, c, first, between):
                g = layer * NC + c
                if layer == 0:
                    pe.wait_ge(gw_ready, 2)
                for f in range(KD):
                    if not first:
                        pe.wait_ge(sum_read, KD * g + (f + 1 - KD))
                    for k in range(KD):
                        for i, (a, b) in enumerate(PASSES):
                            mm(psum[:, SUM[f], :], gwp[:, layer, a, k, f * P:(f + 1) * P],
                               acts(c, b, k), start=(k == 0 and i == 0), stop=False)
                pe.wait_ge(u_lo, (layer + 1) * (NT // 2))
                if layer == 0 and not first:
                    pe.wait_ge(adj_lo, c * GPC + GPC)
                for f in range(KD):
                    for j in range(NT):
                        if first and f == 0 and j % JB == 0:
                            pe.wait_ge(adj_lo, (j // JB + 1) * TPC)
                        for i, (a, b) in enumerate(PASSES):
                            last = mm(psum[:, SUM[f], :], u[:, a, j, f * P:(f + 1) * P],
                                      adj_t[:, bass.ds(c, 1), b, j, :].rearrange("p a w -> p (a w)"),
                                      start=False, stop=(j == NT - 1 and i == 2))
                        if j == NT - 1:
                            last.then_inc(sum_mm, 1)
                        for work in between.get((f, j), ()):
                            work()

            start_order(lambda c: None, x_chunk, lambda n: rows_times_w(0, n), lambda g: transpose_group(0, g, True))

            def with_next(c):
                return {(i // NT, i % NT): [lambda g=i // 2: transpose_group(c + 1, g, False)]
                        for i in range(0, KD * NT, 2)}

            beside = {(0, j): [] for j in range(GPC - AHEAD - 2)}
            for g in range(AHEAD, GPC):
                j = max(g - AHEAD - 2, (g - AHEAD) // 2)
                beside[(0, j)].append(lambda g=g: transpose_group(0, g, True))
            beside.update({(1, j): [lambda g=j: transpose_group(1, g, False)] for j in range(GPC)})
            chunk(0, 0, True, beside)
            with pe.Fori(1, NC - 1) as c:
                chunk(0, c, False, with_next(c))
            chunk(0, NC - 1, False, {})
            for n in range(NT // 2):
                rows_times_w(1, n)

            def o_back(c, first):
                pe.wait_ge(o_ready, KD * c + KD)
                for b in range(2):
                    if not first:
                        pe.wait_ge(y_ready, 2 * c + (b - 1))
                    for q in (2 * b, 2 * b + 1):
                        for f in range(KD):
                            at = (q % 2) * D + f * P
                            last = nc.tensor.transpose(psum[:, OT[b], at:at + P],
                                                       sum_2[:, f, q * P:(q + 1) * P], ident[:])
                    last.then_inc(o_tp, 1)

            def xn2_transposes(c):
                for b in range(2):
                    pe.wait_ge(row_ready, 2 * c + (b + 1))
                    for q in (2 * b, 2 * b + 1):
                        for k in range(KD):
                            at = (q % 2) * D + k * P
                            last = nc.tensor.transpose(psum[:, XT[b], at:at + P],
                                                       row[0][:, q, k * P:(k + 1) * P], ident[:])
                    last.then_inc(xn2_tp, 1)

            def gate_logits(c, first):
                if not first:
                    pe.wait_ge(gate_read, c)
                for q in range(TPC):
                    if q % 2 == 0:
                        pe.wait_ge(xn2_copied, 2 * c + (q // 2 + 1))
                    for k in range(KD):
                        last = mm(psum[:, GATE, q * E:(q + 1) * E], xn2_t[:, (q * KD + k) * P:(q * KD + k + 1) * P],
                                  wg_sb[:, k, :], start=(k == 0), stop=(k == KD - 1))
                last.then_inc(logits_mm, 1)

            def ranks(c):
                pe.wait_ge(mask_ready, c + 1)
                o = psum[:, GATE, 64:64 + TPC * E].rearrange("p (q e) -> p q e", q=TPC)
                mm(o, before[:], mask, start=True, stop=False)
                mm(o, ones[:], carry.unsqueeze(1).to_broadcast([P, TPC, E]), start=False, stop=False)
                for d in range(1, TPC):
                    last = mm(o[:, d:, :], ones[:], mask[:, 0:TPC - d, :], start=False, stop=(d == TPC - 1))
                last.then_inc(rank_mm, 1)

            def tail(c, first):
                return {(0, 0): [lambda: o_back(c, first)],
                        (0, 13): [lambda: xn2_transposes(c)],
                        (1, 1): [lambda: gate_logits(c, first)],
                        (1, 8): [lambda: ranks(c)]}

            chunk(1, 0, False, {})
            chunk(1, 1, False, tail(0, True))
            with pe.Fori(2, NC) as c:
                chunk(1, c, False, tail(c - 1, False))
            o_back(NC - 1, False)
            xn2_transposes(NC - 1)
            gate_logits(NC - 1, False)
            ranks(NC - 1)
            pe.wait_ge(carried, NC)
            mm(psum[:, COUNT, 0:E], ones[:], carry, start=True, stop=True).then_inc(count_mm, 1)

            def x_transposes(t, s, nth, first=False):
                pe.wait_ge(xin_arrived[s], 16 * nth + 16)
                if not first:
                    pe.wait_ge(fx_lo, t)
                for k in range(KD):
                    last = nc.tensor.transpose(psum[:, FX, k * P:(k + 1) * P],
                                               x_in[:, s, k * P:(k + 1) * P], ident[:])
                last.then_inc(fx_tp, 1)

            def hidden(t, place, m, first=False):
                if m == 0:
                    pe.wait_ge(fx_lo, t + 1)
                for i, (lo, _) in enumerate(HG):
                    if m == lo and not first:
                        pe.wait_ge(silu_ready, 2 * t + (i - 1))
                        pe.wait_ge(gated_ready, 2 * t + (i - 1))
                n = 0
                for k in range(KD):
                    for b, parts in ((HI, (HI, LO)), (LO, (HI,))):
                        w = big[:, bass.ds(place + ((k * 2 + b) * NP + m) * CW, CW)]
                        for a in parts:
                            last = mm(psum[:, m, :], x_part[:, a, k * P:(k + 1) * P], w,
                                      start=(n == 0), stop=(n == 3 * KD - 1))
                            n += 1
                if m + 1 in (HG[0][1], HG[1][1]):
                    last.then_inc(hg_mm, 1)

            def act_transposes(t, first=False):
                pe.wait_ge(act_ready, t + 1)
                for b, fs in enumerate((range(0, 4), range(4, KF))):
                    if not first:
                        pe.wait_ge(fa_lo, 2 * t + (b - 1))
                    for f in fs:
                        last = nc.tensor.transpose(psum[:, FA[b], (f % 4) * P:(f % 4 + 1) * P],
                                                   act_f[:, f * P:(f + 1) * P], ident[:])
                    last.then_inc(fa_tp, 1)

            def down(t, place, first=False):
                if not first:
                    pe.wait_ge(fy_ready, t)
                n = 0
                for f in range(KF):
                    if f == 0:
                        pe.wait_ge(fa_lo, 2 * t + 1)
                    if f == 4:
                        pe.wait_ge(fa_lo, 2 * t + 2)
                    for b, parts in ((HI, (HI, LO)), (LO, (HI,))):
                        w = big[:, bass.ds(place + (W13 + (f * 2 + b) * D), D)]
                        for a in parts:
                            last = mm(psum[:, FY, 0:D], act_part[:, a, f * P:(f + 1) * P], w,
                                      start=(n == 0), stop=(n == 3 * KF - 1))
                            n += 1
                last.then_inc(fy_mm, 1)

            def place_of(t):
                return pe.value_load(table[:, 1, bass.ds(t, 1)], min_val=0, max_val=(E - 1) * EW)

            def first_tile():
                pe.wait_ge(table_ready, 1)
                pe.wait_ge(piece_lo, E * PIECES)
                x_transposes(0, 0, 0, first=True)
                p = place_of(0)
                for m in range(NP):
                    hidden(0, p, m, first=True)
                x_transposes(1, 1, 0)

            def tile(t, s, nth, more, fresh):
                p = place_of(t)
                hidden(t, p, 0)
                act_transposes(t - 1, first=isinstance(t, int) and t == 1)
                hidden(t, p, 1)
                hidden(t, p, 2)
                if more:
                    s1 = (s + 1) % UN
                    x_transposes(t + 1, s1, nth + (1 if s1 == 0 else 0))
                down(t - 1, place_of(t - 1))

            def last_tile(t, s):
                act_transposes(t)
                down(t, place_of(t))

            ffn_tiles(pe, first_tile, tile, last_tile)

        @block.scalar
        def _(act):
            def ln_std(out_ap, var_ap):
                return nc.scalar.activation(out_ap, var_ap, ACT.Sqrt, bias=eps)

            def high(dst, src, scale):
                return nc.scalar.activation(dst, src, ACT.Copy, scale=scale)

            raw_w = gw_raw.rearrange("p (l k d) -> p l k d", l=2, k=2 * KD)
            for layer, w in enumerate((gnn_w1, gnn_w2)):
                act.dma_start(raw_w[:, layer, :, :], w.rearrange("(k p) d -> p k d", p=P)).then_inc(gw_arrived[layer], 16)
            with nc.allow_non_contiguous_dma(reason="two short bias vectors and the gate"):
                for layer, b in enumerate((gnn_b1, gnn_b2)):
                    act.dma_start(bias[:, layer, :], b.rearrange("(k p) -> p k", p=P)).then_inc(small_in, 16)
                act.dma_start(wg_sb, wg.rearrange("(k p) e -> p k e", p=P)).then_inc(small_in, 16)
            act.wait_ge(consts, 1)

            def table_load(function):
                nc.scalar.activation(scratch, eps, function)

            table_load(ACT.Sqrt)

            def normalize(c):
                ts = slice(TPC * c, TPC * (c + 1))
                act.wait_ge(var_1, c + 1)
                ln_std(std_1[:, ts], mv_1[:, ts, 1]).then_inc(std_1_ready, 1)
                act.wait_ge(scaled_1, c + 1)
                for t in range(TPC * c + TPC // 2, TPC * (c + 1)):
                    ins = nc.scalar.activation(xn_all[:, t, :], x_all[:, t, :], ACT.Identity,
                                               scale=rstd_1[:, t:t + 1], bias=shift_1[:, t:t + 1])
                ins.then_inc(xn_act, 1)

            def x_high_1(c):
                for k in range(KD):
                    n = KD * c + k
                    act.wait_ge(xt_tp, n + 1)
                    high(acts(c, HI, k), psum[:, TP[n % 4], :], S_ACT).then_inc(xt_hi, 1)

            def u_high(layer, n):
                act.wait_ge(u_mm, layer * (NT // 2) + n + 1)
                high(u[:, HI, 2 * n:2 * n + 2, :].rearrange("p j d -> p (j d)"), psum[:, UB[n % 2], :],
                     S_ACT / S_SUM).then_inc(u_hi, 1)

            def block_high(c, g, first=False):
                r, jq = block_of(g, first)
                act.wait_ge(adj_tp, c * GPC + (g + 1))
                high(adj_t[:, bass.ds(c, 1), HI, JB * jq:JB * (jq + 1), r * P:(r + 1) * P].rearrange(
                         "p a j w -> p (a j) w"),
                     psum[:, TP[g % 4], :].rearrange("p (j w) -> p j w", j=JB), S_W).then_inc(adj_hi, 1)

            def relu_1(c, f, first):
                if not first:
                    act.wait_ge(h_parts, KD * c + (f + 1 - KD))
                act.wait_ge(sum_mm, KD * c + (f + 1))
                nc.scalar.activation(sum_1[:, f, :], psum[:, SUM[f], :], ACT.Relu, scale=S_ACT / S_SUM,
                                     bias=bias_h[:, f:f + 1]).then_inc(sum_read, 1)

            start_order(normalize, x_high_1, lambda n: u_high(0, n), lambda g: block_high(0, g, True))

            def layer_1(c, first, more):
                for f in range(KD):
                    if more:
                        for g in range(f * GPC // 2, (f + 1) * GPC // 2):
                            block_high(c + 1, g)
                    relu_1(c, f, first)

            for g in range(AHEAD, GPC):
                block_high(0, g, True)
            act.wait_ge(bias_ready, 1)
            relu_1(0, 0, True)
            for g in range(GPC):
                block_high(1, g)
            relu_1(0, 1, True)
            act.wait_ge(gw_ready, 3)
            with act.Fori(1, NC - 1) as c:
                layer_1(c, False, True)
            layer_1(NC - 1, False, False)
            for n in range(NT // 2):
                u_high(1, n)

            def relu_2(c, f):
                act.wait_ge(sum_mm, KD * c + (KD * NC + f + 1))
                nc.scalar.activation(sum_2[:, f, :], psum[:, SUM[f], :], ACT.Relu, scale=1.0 / S_SUM,
                                     bias=bias[:, 1, f:f + 1]).then_inc(sum_read, 1)

            def load_x(c):
                act.dma_start(y_ch, x_t[:, bass.ds(c * TPC, TPC), :]).then_inc(x_again, 16)

            def piece_high(pair, m):
                act.wait_ge(piece_arrived[m % SLOTS], 32 * PIECES // SLOTS * pair + 16 * (m // SLOTS + 1))
                high(expert_piece(2 * pair + m // PIECES, m % PIECES, HI),
                     arriving[m % SLOTS].rearrange("p (a d) -> p a d", a=NP), S_W).then_inc(piece_hi, 1)

            def tail(c, pair, more, before_std, before_gate, before_weights):
                if more:
                    table_load(ACT.Sqrt)
                for m in range(before_std):
                    piece_high(pair, m)
                act.wait_ge(var_2, c + 1)
                ln_std(std_2, mv_2[:, :, 1]).then_inc(std_2_ready, 1)
                act.wait_ge(y_ready, 2 * c + 2)
                act.dma_start(total_t[:, bass.ds(c * TPC, TPC), :], y_ch).then_inc(y_stored, 16)
                for m in range(before_std, before_gate):
                    piece_high(pair, m)
                for b in range(2):
                    act.wait_ge(xn2_tp, 2 * c + (b + 1))
                    nc.scalar.copy(xn2_t[:, b * CW:(b + 1) * CW], psum[:, XT[b], :]).then_inc(xn2_copied, 1)
                act.wait_ge(row_ready, 2 * c + 2)
                nc.scalar.copy(row[1][:, :, 0:D], row[0][:, :, 0:D]).then_inc(row_copied, 1)
                if not more:
                    act.wait_ge(o_ready, KD * NC)
                    act.dma_start(b3_all[:, b3_early * F:], b3[b3_early:E, :].rearrange("e f -> (e f)").partition_broadcast(P)
                                  ).then_inc(b3_arrived, 16)
                table_load(ACT.Exp)
                for m in range(before_gate, before_weights):
                    piece_high(pair, m)
                if more:
                    act.wait_ge(y_stored, 16 * c + 16)
                    load_x(c + 1)
                    act.wait_ge(logits_mm, c + 1)
                    relu_2(c + 1, 0)
                act.wait_ge(gap_ready, c + 1)
                nc.scalar.activation(expd, gap, ACT.Exp).then_inc(exp_ready, 1)
                if not more:
                    act.wait_ge(pads_known, 1)
                    act.wait_ge(pad_built, 1)
                    for e in range(E - 2, E):
                        store_pad(act, e)
                for m in range(before_weights, 2 * PIECES - 2):
                    piece_high(pair, m)
                    if not more and PIECES <= m < 2 * PIECES - SLOTS:
                        load_last(act, m - PIECES + SLOTS)
                if more:
                    relu_2(c + 1, 1)
                for m in range(2 * PIECES - 2, 2 * PIECES):
                    piece_high(pair, m)

            act.wait_ge(adj_tp, NC * GPC)
            load_x(0)
            for f in range(KD):
                relu_2(0, f)
            with act.Fori(0, NC - 1) as c:
                tail(c, c, True, 1, 5, 7)
            table_load(ACT.Sqrt)
            tail(NC - 1, NC - 1, False, 0, 3, 4)
            table_load(ACT.Silu)

            def x_high(t):
                act.wait_ge(fx_tp, t + 1)
                high(x_part[:, HI, :], psum[:, FX, 0:D], S_ACT).then_inc(fx_hi, 1)

            def silu(t, first=False):
                if not first:
                    act.wait_ge(act_ready, t)
                for i, (lo, hi) in enumerate(HG):
                    act.wait_ge(hg_mm, 2 * t + (i + 1))
                    nc.scalar.activation(silu_h[:, lo * FP:hi * FP].rearrange("p (m w) -> p m w", w=FP),
                                         psum[:, lo:hi, 0:FP], ACT.Silu, scale=1.0 / S_SUM
                                         ).then_inc(silu_ready, 1)

            def act_high(t):
                for b, (lo, hi) in enumerate(((0, CW), (CW, F))):
                    act.wait_ge(fa_tp, 2 * t + (b + 1))
                    high(act_part[:, HI, lo:hi], psum[:, FA[b], 0:hi - lo], 1.0).then_inc(fa_hi, 1)

            def first_tile():
                x_high(0)
                silu(0, first=True)
                x_high(1)

            def tile(t, s, nth, more, fresh):
                act_high(t - 1)
                silu(t)
                if more:
                    x_high(t + 1)

            ffn_tiles(act, first_tile, tile, lambda t, s: act_high(t))

        @block.vector
        def _(dve):
            step = Steps(dve, dve_step)
            v = nc.vector

            def low(dst, src, scale, hi_part):
                return v.scalar_tensor_tensor(out=dst, in0=src, scalar=scale, in1=hi_part,
                                              op0=ALU.mult, op1=ALU.subtract)

            def layernorm_stats(src, st, mv, n):
                for q in range(n):
                    ins = v.bn_stats(st[:, q, :], src[:, q, :])
                step.wait_for(ins)
                for q in range(n):
                    ins = v.bn_aggr(mv[:, q, :], st[:, q, :])
                return ins

            def stats(c):
                ts = slice(TPC * c, TPC * (c + 1))
                dve.wait_ge(x_arrived[c], 16)
                layernorm_stats(x_all[:, ts, :], st_1[:, ts, :], mv_1[:, ts, :], TPC).then_inc(var_1, 1)

            def normalize(c):
                ts = slice(TPC * c, TPC * (c + 1))
                dve.wait_ge(std_1_ready, c + 1)
                step.wait_for(v.reciprocal(rstd_1[:, ts], std_1[:, ts]))
                v.scalar_tensor_tensor(out=shift_1[:, ts], in0=mv_1[:, ts, 0], scalar=-1.0, in1=rstd_1[:, ts],
                                       op0=ALU.mult, op1=ALU.mult).then_inc(scaled_1, 1)
                for t in range(TPC * c, TPC * c + TPC // 2):
                    ins = v.tensor_scalar(xn_all[:, t, :], x_all[:, t, :], mv_1[:, t, 0:1], rstd_1[:, t:t + 1],
                                          ALU.subtract, ALU.mult)
                ins.then_inc(xn_dve, 1)
                if c + 2 < NC:
                    stats(c + 2)

            def x_low_1(c):
                for k in range(KD):
                    n = KD * c + k
                    dve.wait_ge(xt_hi, n + 1)
                    low(acts(c, LO, k), psum[:, TP[n % 4], :], S_ACT, acts(c, HI, k)).then_inc(xt_lo, 1)

            def u_low(layer, n):
                dve.wait_ge(u_hi, layer * (NT // 2) + n + 1)
                low(u[:, LO, 2 * n:2 * n + 2, :].rearrange("p j d -> p (j d)"), psum[:, UB[n % 2], :],
                    S_ACT / S_SUM, u[:, HI, 2 * n:2 * n + 2, :].rearrange("p j d -> p (j d)")
                    ).then_inc(u_lo, 1)

            def block_low(c, g, first=False):
                r, jq = block_of(g, first)
                dve.wait_ge(adj_hi, c * GPC + (g + 1))
                hi, lo = (adj_t[:, bass.ds(c, 1), h, JB * jq:JB * (jq + 1), r * P:(r + 1) * P].rearrange(
                    "p a j w -> p (a j) w") for h in (HI, LO))
                low(lo, psum[:, TP[g % 4], :].rearrange("p (j w) -> p j w", j=JB), S_W, hi).then_inc(adj_lo, 1)

            def h_split(c, f):
                dve.wait_ge(sum_read, KD * c + (f + 1))
                step.wait_for(v.tensor_copy(acts(c, HI, f), sum_1[:, f, :]))
                v.tensor_tensor(acts(c, LO, f), sum_1[:, f, :], acts(c, HI, f),
                                ALU.subtract).then_inc(h_parts, 1)

            stats(0)
            stats(1)
            start_order(normalize, x_low_1, lambda n: u_low(0, n), lambda g: block_low(0, g, True))

            def layer_1(c, more):
                for f in range(KD):
                    if more:
                        for g in range(f * GPC // 2, (f + 1) * GPC // 2):
                            block_low(c + 1, g)
                    h_split(c, f)

            for g in range(AHEAD, GPC):
                block_low(0, g, True)
            dve.wait_ge(small_in, 48)
            v.tensor_scalar(bias_h, bias[:, 0, :], S_ACT, None, ALU.mult).then_inc(bias_ready, 1)
            h_split(0, 0)
            for g in range(GPC):
                block_low(1, g)
            h_split(0, 1)
            dve.wait_ge(gw_ready, 3)
            base = step.n
            with dve.Fori(1, NC - 1) as c:
                step.base, step.n = base + (c - 1) * KD, 0
                layer_1(c, True)
            step.base, step.n = base + (NC - 2) * KD, 0
            layer_1(NC - 1, False)
            for n in range(NT // 2):
                u_low(1, n)

            def add_h(c, f):
                dve.wait_ge(sum_read, KD * c + (KD * NC + f + 1))
                step.wait_for(v.scalar_tensor_tensor(
                    out=sum_2[:, f, :], in0=acts(c, LO, f), scalar=1.0 / S_ACT, in1=sum_2[:, f, :],
                    op0=ALU.mult, op1=ALU.add))
                v.scalar_tensor_tensor(
                    out=sum_2[:, f, :], in0=acts(c, HI, f), scalar=1.0 / S_ACT, in1=sum_2[:, f, :],
                    op0=ALU.mult, op1=ALU.add).then_inc(o_ready, 1)

            def piece_low(pair, m):
                dve.wait_ge(piece_hi, 2 * PIECES * pair + (m + 1))
                e, n = 2 * pair + m // PIECES, m % PIECES
                low(expert_piece(e, n, LO), arriving[m % SLOTS].rearrange("p (a d) -> p a d", a=NP), S_W,
                    expert_piece(e, n, HI)).then_inc(piece_lo, 1)

            def tail(c, pair, first, more, cuts):
                def pieces(i):
                    for m in range(([0] + cuts)[i], cuts[i]):
                        piece_low(pair, m)

                pieces(0)
                dve.wait_ge(x_again, 16 * c + 16)
                for b in range(2):
                    dve.wait_ge(o_tp, 2 * c + (b + 1))
                    y2 = y_ch[:, 2 * b:2 * b + 2, :].rearrange("p q d -> p (q d)")
                    v.scalar_tensor_tensor(out=y2, in0=psum[:, OT[b], :], scalar=0.0, in1=y2,
                                           op0=ALU.max, op1=ALU.add).then_inc(y_ready, 1)
                dve.wait_ge(y_ready, 2 * c + 2)
                layernorm_stats(y_ch, st_2, mv_2, TPC).then_inc(var_2, 1)
                pieces(1)
                dve.wait_ge(std_2_ready, c + 1)
                step.wait_for(v.reciprocal(rstd_2, std_2))
                if not first:
                    dve.wait_ge(scattered, c * (16 * TPC * TOP))
                for q in range(TPC):
                    ins = v.tensor_scalar(row[0][:, q, 0:D], y_ch[:, q, :], mv_2[:, q, 0:1], rstd_2[:, q:q + 1],
                                          ALU.subtract, ALU.mult)
                    if q % 2:
                        ins.then_inc(row_ready, 1)
                pieces(2)
                dve.wait_ge(logits_mm, c + 1)
                step.wait_for(v.tensor_copy(logits, psum[:, GATE, 0:TPC * E].rearrange("p (q e) -> p q e", q=TPC)))
                for q in range(TPC):
                    ins = v.max(best[:, q, :], logits[:, q, :])
                step.wait_for(ins)
                v.tensor_tensor(gap, best[:, :, 1], best[:, :, 0], ALU.subtract).then_inc(gap_ready, 1)
                for q in range(TPC):
                    ins = v.max_index(best_ix[:, q, :], best[:, q, :], logits[:, q, :])
                step.wait_for(ins)
                step.wait_for(v.tensor_copy(choice, best_ix[:, :, 0:TOP]))
                pick = small["choice"].unsqueeze(2).to_broadcast([P, TPC * TOP, E])
                step.wait_for(v.tensor_tensor(
                    small["onehot"].rearrange("p (i e) -> p i e", e=E), pick,
                    iota_e.unsqueeze(1).to_broadcast([P, TPC * TOP, E]), ALU.is_equal))
                v.tensor_tensor(mask, onehot[:, :, 0, :], onehot[:, :, 1, :], ALU.add).then_inc(mask_ready, 1)
                pieces(3)
                dve.wait_ge(exp_ready, c + 1)
                step.wait_for(v.tensor_scalar(den, expd, 1.0, None, ALU.add))
                step.wait_for(v.reciprocal(row[0][:, :, D], den))
                v.tensor_tensor(row[1][:, :, D], expd, row[0][:, :, D], ALU.mult).then_inc(weights_ready, 1)
                dve.wait_ge(rank_mm, c + 1)
                v.tensor_tensor(place, psum[:, GATE, 64:64 + TPC * E].rearrange("p (q e) -> p q e", q=TPC),
                                region_0.unsqueeze(1).to_broadcast([P, TPC, E]), ALU.add).then_inc(gate_read, 1)
                with nc.allow_low_precision(reason="counts up to 16"):
                    step.wait_for(v.tensor_reduce(added, mask.rearrange("p q e -> p e q"), AX_X, ALU.add))
                v.tensor_tensor(carry, carry, added, ALU.add).then_inc(carried, 1)
                dve.wait_ge(gate_read, c + 1)
                for k in range(TOP):
                    ins = v.tensor_tensor(picked[:, :, k, :], onehot[:, :, k, :], place, ALU.mult)
                step.wait_for(ins)
                step.wait_for(v.tensor_reduce(slot_f, small["picked"].rearrange("p (i e) -> p i e", e=E),
                                              AX_X, ALU.add))
                v.tensor_copy(slot, slot_f).then_inc(slots_ready, 1)
                if more:
                    pieces(4)
                    add_h(c + 1, 0)
                    pieces(5)
                    add_h(c + 1, 1)
                    pieces(6)

            for f in range(KD):
                add_h(0, f)
            for c in range(NC):
                tail(c, c, c == 0, c < NC - 1, [1, 1, 6, 7, 10, 10, 12] if c < NC - 1 else [0, 0, 4, 4])

            dve.wait_ge(late_consts, 1)
            dve.wait_ge(count_mm, 1)
            step.wait_for(v.tensor_copy(n_e, psum[0:1, COUNT, 0:E]))
            step.wait_for(v.tensor_tensor(pad_f, n_e, region_0[0:1, :], ALU.add))
            v.tensor_copy(pad_row, pad_f).then_inc(pads_known, 1)
            for m in range(4, 7):
                piece_low(NC - 1, m)
            step.wait_for(v.tensor_tensor(over_k, n_e.unsqueeze(2).to_broadcast([1, E, NT]),
                                          iota_k.unsqueeze(1).to_broadcast([1, E, NT]), ALU.is_gt))
            step.wait_for(v.tensor_reduce(nt_e, over_k, AX_X, ALU.add))
            v.memset(delta[:, 0:1], 0.0)
            v.tensor_scalar(delta[:, 1:E], nt_e[:, 0:E - 1], -float(P), float(REG), ALU.mult, ALU.add)
            step.wait_for(v.tensor_tensor(over_e, nt_e.unsqueeze(1).to_broadcast([1, E, E]), upto, ALU.mult))
            step.wait_for(v.tensor_reduce(last, over_e, AX_X, ALU.add))
            step.wait_for(v.tensor_tensor(first, last, nt_e, ALU.subtract))
            step.wait_for(v.tensor_tensor(started, iota_n.unsqueeze(2).to_broadcast([1, TILES, E]),
                                          first.unsqueeze(1).to_broadcast([1, TILES, E]), ALU.is_ge))
            v.tensor_reduce(experts_seen, started, AX_X, ALU.add)
            step.wait_for(v.tensor_tensor(shifts, started, delta.unsqueeze(1).to_broadcast([1, TILES, E]), ALU.mult))
            step.wait_for(v.tensor_reduce(row_shift, shifts, AX_X, ALU.add))
            step.wait_for(v.scalar_tensor_tensor(out=tab_f[:, 0, :], in0=iota_n, scalar=float(P), in1=row_shift,
                                                 op0=ALU.mult, op1=ALU.add))
            v.tensor_scalar(tab_f[:, 0, :], tab_f[:, 0, :], pad_f[:, E - 1:E], None, ALU.min)
            v.tensor_scalar(tab_f[:, 1, :], experts_seen, float(EW), -float(EW), ALU.mult, ALU.add)
            step.wait_for(v.tensor_scalar(tab_f[:, 2, :], experts_seen, float(F), -float(F), ALU.mult, ALU.add))
            v.tensor_copy(table, tab_f).then_inc(table_ready, 1)
            for m in range(7, 2 * PIECES):
                piece_low(NC - 1, m)

            def token_copy(t, s, nth, fresh):
                dve.wait_ge(xin_arrived[s], 16 * nth + 16)
                if not fresh:
                    dve.wait_ge(fy_added, 16 * t + 16 * (1 - UN))
                v.tensor_copy(token_w[:, s:s + 1], x_in[:, s, D:D + 1])
                v.tensor_copy(token_ix[:, s:s + 1], x_in[:, s, D + 1:D + 2]).then_inc(token_read, 1)

            def x_low(t):
                dve.wait_ge(fx_hi, t + 1)
                low(x_part[:, LO, :], psum[:, FX, 0:D], S_ACT, x_part[:, HI, :]).then_inc(fx_lo, 1)

            def gate_g(t, first=False):
                b = dve.value_load(table[:, 2, bass.ds(t, 1)], min_val=0, max_val=(E - 1) * F)
                for i, (lo, hi) in enumerate(HG):
                    dve.wait_ge(silu_ready, 2 * t + (i + 1))
                    v.scalar_tensor_tensor(out=gated[:, lo * FP:hi * FP].rearrange("p (m w) -> p m w", w=FP),
                                           in0=psum[:, lo:hi, FP:2 * FP], scalar=1.0 / S_SUM,
                                           in1=b3_all[:, bass.ds(b + lo * FP, (hi - lo) * FP)].rearrange(
                                               "p (m w) -> p m w", w=FP), op0=ALU.mult, op1=ALU.add
                                           ).then_inc(gated_ready, 1)

            def activate(t, first=False):
                dve.wait_ge(gated_ready, 2 * t + 2)
                if not first:
                    dve.wait_ge(fa_tp, 2 * t)
                v.scalar_tensor_tensor(out=act_f, in0=gated, scalar=S_ACT, in1=silu_h,
                                       op0=ALU.mult, op1=ALU.mult).then_inc(act_ready, 1)

            def act_low(t):
                for b, (lo, hi) in enumerate(((0, CW), (CW, F))):
                    dve.wait_ge(fa_hi, 2 * t + (b + 1))
                    v.tensor_tensor(act_part[:, LO, lo:hi], psum[:, FA[b], 0:hi - lo], act_part[:, HI, lo:hi],
                                    ALU.subtract).then_inc(fa_lo, 1)

            def y_weigh(t, s):
                dve.wait_ge(fy_mm, t + 1)
                dve.wait_ge(token_read, t + 1)
                v.tensor_scalar(y_out[:, s, :], psum[:, FY, 0:D], token_w[:, s:s + 1], 1.0 / S_SUM,
                                ALU.mult, ALU.mult).then_inc(fy_ready, 1)

            def first_tile():
                dve.wait_ge(b3_early_in, 16)
                dve.wait_ge(b3_arrived, 16)
                dve.wait_ge(table_ready, 1)
                x_low(0)
                token_copy(0, 0, 0, fresh=True)
                gate_g(0)
                x_low(1)
                activate(0, first=True)

            def tile(t, s, nth, more, fresh):
                act_low(t - 1)
                token_copy(t, s, nth, fresh)
                gate_g(t)
                if more:
                    x_low(t + 1)
                activate(t)
                y_weigh(t - 1, (s - 1) % UN)

            def last_tile(t, s):
                act_low(t)
                y_weigh(t, s)

            ffn_tiles(dve, first_tile, tile, last_tile)


_INS = ['x', 'adj', 'L0_gnn_W1', 'L0_gnn_b1', 'L0_gnn_W2', 'L0_gnn_b2', 'L0_ffn_Wg', 'L0_ffn_W1',
        'L0_ffn_W2', 'L0_ffn_W3', 'L0_ffn_b3']
_OUTS = [((2048, 256), 'float32')]


def kernel(**inputs):
    import numpy as _np
    import concourse.bacc as _bacc
    from concourse import mybir as _mybir
    from concourse.bass_utils import run_bass_kernel_spmd as _run

    nc = _bacc.Bacc("TRN2", target_bir_lowering=False, num_devices=1)
    arrays, args = {}, []
    for name in _INS:
        a = _np.ascontiguousarray(inputs[name])
        arrays[f"in_{name}_dram"] = a
        args.append(nc.dram_tensor(f"in_{name}_dram", a.shape, _mybir.dt.from_np(a.dtype), kind="ExternalInput").ap())
    for i, (shape, dtype) in enumerate(_OUTS):
        dt = _mybir.dt.from_np(_np.dtype(dtype))
        args.append(nc.dram_tensor(f"out_{i}_dram", shape, dt, kind="ExternalOutput").ap())
    moe_gnn_kernel(nc, *args)
    r = _run(nc, [arrays], core_ids=[0])
    got = tuple(r.results[0][f"out_{i}_dram"] for i in range(len(_OUTS)))
    return got[0]
```

```python
from contextlib import ExitStack

import concourse.bass as bass
from concourse import mybir

P = 128
F32, F16 = mybir.dt.float32, mybir.dt.float16
I32, U32 = mybir.dt.int32, mybir.dt.uint32
ALU = mybir.AluOpType
ACT = mybir.ActivationFunctionType
AX_X = mybir.AxisListType.X

S_ACT = 16.0
S_W = 1024.0
S_SUM = S_ACT * S_W
EPS = 1e-5
HI, LO = 0, 1
PASSES = ((HI, HI), (LO, HI), (HI, LO))
TOP = 2


class Steps:

    def __init__(self, eng, sem):
        self.eng, self.sem, self.base, self.n = eng, sem, 0, 0

    def wait_for(self, ins):
        self.n += 1
        ins.then_inc(self.sem, 1)
        self.eng.wait_ge(self.sem, self.base + self.n)


def moe_gnn_kernel(nc, x, adj, gnn_w1, gnn_b1, gnn_w2, gnn_b2, wg, w1, w2, w3, b3, out):
    N, D = x.shape
    E, _, F = w1.shape
    NT, KD, KF = N // P, D // P, F // P
    CW = 512
    NC, TPC = N // CW, CW // P
    JB = CW // P
    GPC = TPC * NT // JB
    GPR = GPC // TPC
    NP = 3
    FP = F // NP
    ROW = D + 2
    REG = N + P
    TILES = TOP * N // P + E - 1
    UN = 3
    W13 = 2 * KD * NP * CW
    EW = W13 + 2 * KF * D
    ADJC = 2 * NT * CW
    EXT = E * EW - NC * ADJC
    PIECES = 2 * KD + 2
    SLOTS, SLOTS_LATE = 3, 6
    FEW_SLOTS = 5 * PIECES
    LAST_BY_SP = 2
    assert 2 * FP == CW and NC == 4 and TPC == 4 and EXT == 4 * N and EW <= ADJC
    assert TILES % UN == 0 and KF == 2 * NP and GPC == NT and E == 2 * NC
    assert FEW_SLOTS % SLOTS_LATE == 0 and 2 * F * (SLOTS_LATE - 2) <= (NC - 1) * 2 * KD * CW
    assert PIECES % SLOTS == 0

    routed = nc.dram_tensor("routed_rows", (E * REG, ROW), F32, kind="Internal").ap()
    total = nc.dram_tensor("row_sums", (N + P, D), F32, kind="Internal").ap()
    x_t = x.rearrange("(t p) d -> p t d", p=P)
    total_t = total.rearrange("(t p) d -> p t d", p=P)

    with ExitStack() as ctx:
        def sb(name, shape, dt):
            return ctx.enter_context(nc.sbuf_tensor(name, shape, dt))

        def sem(name):
            return ctx.enter_context(nc.semaphore(name))

        big = sb("big", [P, E * EW], F16)
        tu = sb("tu", [P, 2 * KD * N + 2 * NT * D], F16)
        rb = sb("rb", [P, 2 * N], F32)
        gw = sb("gw", [P, 2 * 2 * 2 * KD * D], F16)
        stage = sb("stage", [P, 2, F], F32)
        ident = sb("ident", [P, P], F32)
        before = sb("before", [P, P], F16)
        ones = sb("ones", [P, P], F16)
        fixed = sb("fixed", [P, 76], F32)
        bias = fixed[:, 0:4].rearrange("p (l k) -> p l k", l=2)
        bias_h = fixed[:, 4:6]
        wg_sb = fixed[:, 6:6 + KD * E].rearrange("p (k e) -> p k e", k=KD)
        eps = fixed[:, 22:23]
        scratch = fixed[:, 23:24]
        iota_e = fixed[:, 24:32]
        region_0 = fixed[:, 32:40]
        token_no = fixed[:, 40:56]
        token_w = fixed[:, 56:56 + UN]
        token_ix = fixed[:, 60:60 + UN].bitcast(U32)
        rstd_2 = fixed[:, 64:68]
        std_2 = fixed[:, 68:72]
        carry = fixed[:, 72:76].bitcast(F16)

        adj_t = big[:, EXT:].rearrange("p (c h j w) -> p c h j w", c=NC, h=2, j=NT)
        low_rows = big[:, 0:EXT].bitcast(F32)
        adj_rows = [low_rows[:, 0:N], low_rows[:, N:2 * N], rb[:, 0:N], rb[:, N:2 * N]]
        late = EXT + (NC - 1) * ADJC
        x_all = big[:, late:late + ADJC // 2].bitcast(F32).rearrange("p (t d) -> p t d", t=NT)
        xn_all = big[:, late + ADJC // 2:].bitcast(F32).rearrange("p (t d) -> p t d", t=NT)
        raw = big[:, late - ADJC:late].bitcast(F32)
        gw_raw = raw[:, 0:4 * KD * D]
        st_1 = raw[:, 4 * KD * D:4 * KD * D + 6 * NT].rearrange("p (t s) -> p t s", t=NT)
        mv_1 = raw[:, 4 * KD * D + 128:4 * KD * D + 128 + 2 * NT].rearrange("p (t s) -> p t s", t=NT)
        std_1 = raw[:, 4 * KD * D + 160:4 * KD * D + 160 + NT]
        rstd_1 = raw[:, 4 * KD * D + 176:4 * KD * D + 176 + NT]
        shift_1 = raw[:, 4 * KD * D + 192:4 * KD * D + 192 + NT]
        act_t = tu[:, 0:2 * KD * N].rearrange("p (c h k w) -> p c h k w", c=NC, h=2, k=KD)
        u = tu[:, 2 * KD * N:].rearrange("p (h j d) -> p h j d", h=2, j=NT)
        gwp = gw[:, :].rearrange("p (l h k d) -> p l h k d", l=2, h=2, k=2 * KD)
        sum_1 = stage[:, :, 0:CW]
        slots_w = [stage[:, 0, :], stage[:, 1, :]]
        slots_w += [tu[:, 2 * F * i:2 * F * (i + 1)].bitcast(F32) for i in range(SLOTS_LATE - 2)]

        def slot_of(m):
            if m < FEW_SLOTS:
                return m % SLOTS, m // SLOTS + 1
            slot = (m - FEW_SLOTS) % SLOTS_LATE
            return slot, (m - FEW_SLOTS) // SLOTS_LATE + 1 + (FEW_SLOTS // SLOTS if slot < SLOTS else 0)

        def split_before(m):
            return m + 1 - (SLOTS if m < FEW_SLOTS + SLOTS else SLOTS_LATE)

        def arriving(m):
            return rb[:, TPC * D:TPC * D + F] if m == 2 else slots_w[slot_of(m)[0]]

        SPLIT = []
        for c in range(NC + 1):
            free_to = E * EW if c == NC else EXT + c * ADJC
            m = 0
            while m < E * PIECES:
                e, n = m // PIECES, m % PIECES
                if n < 2 * KD:
                    end = (n % KD + 1) * (W13 // KD)
                else:
                    end = W13 + (n - 2 * KD + 1) * (2 * KF * D // 2)
                if e * EW + end > free_to:
                    break
                m += 1
            SPLIT.append(m)
        SPLIT[1] -= 1
        SPLIT[NC - 1] -= 1
        sum_2 = gw[:, 0:2 * 2 * KD * D].bitcast(F32).rearrange("p (f w) -> p f w", f=KD)
        xn2_t = gw[:, 0:2 * 2 * KD * D].bitcast(F32)

        y_ch = rb[:, 0:TPC * D].rearrange("p (q d) -> p q d", q=TPC)
        at = TPC * D
        row = []
        for k in range(TOP):
            row.append(rb[:, at:at + TPC * ROW].rearrange("p (q d) -> p q d", q=TPC))
            at += TPC * ROW
        small = {}
        for name, n in (("st_2", 24), ("mv_2", 8), ("logits", 32), ("best", 32), ("best_ix", 32),
                        ("choice", 8), ("onehot", 64), ("place", 32), ("picked", 64),
                        ("slot_f", 8), ("slot", 8), ("gap", 4), ("expd", 4), ("den", 4),
                        ("mask", 16), ("added", 4)):
            small[name] = rb[:, at:at + n]
            at += n
        st_2 = small["st_2"].rearrange("p (q s) -> p q s", q=TPC)
        mv_2 = small["mv_2"].rearrange("p (q s) -> p q s", q=TPC)
        logits = small["logits"].rearrange("p (q e) -> p q e", q=TPC)
        best = small["best"].rearrange("p (q e) -> p q e", q=TPC)
        best_ix = small["best_ix"].bitcast(U32).rearrange("p (q e) -> p q e", q=TPC)
        choice = small["choice"].rearrange("p (q k) -> p q k", q=TPC)
        onehot = small["onehot"].rearrange("p (q k e) -> p q k e", q=TPC, k=TOP)
        picked = small["picked"].rearrange("p (q k e) -> p q k e", q=TPC, k=TOP)
        place = small["place"].rearrange("p (q e) -> p q e", q=TPC)
        slot_f, slot = small["slot_f"], small["slot"].bitcast(U32)
        gap, expd, den = small["gap"], small["expd"], small["den"]
        mask = small["mask"].bitcast(F16).rearrange("p (q e) -> p q e", q=TPC)
        added = small["added"].bitcast(F16)
        iota_k = rb[0:1, at:at + NT]
        upto = rb[0:1, at + 16:at + 80].rearrange("p (a b) -> p a b", a=E)
        iota_n = rb[0:1, at + 80:at + 80 + TILES]
        cnt = rb[0:1, at + 120:at + 120 + 8 * E]
        n_e, nt_e, last, first, delta, pad_f = (cnt[:, E * i:E * i + E] for i in range(6))
        pad_row = cnt[:, 6 * E:7 * E].bitcast(I32)
        experts_seen = rb[0:1, at + 184:at + 184 + TILES]
        row_shift = rb[0:1, at + 224:at + 224 + TILES]
        tab_f = rb[0:1, at + 264:at + 264 + 3 * TILES].rearrange("p (a t) -> p a t", a=3)
        assert at + 264 + 3 * TILES <= 2 * N
        wide = gw[0:1, 0:4 * KD * D].bitcast(F32)
        over_k = wide[:, 0:E * NT].rearrange("p (e k) -> p e k", e=E)
        over_e = wide[:, 128:128 + E * E].rearrange("p (a b) -> p a b", a=E)
        started = wide[:, 192:192 + E * TILES].rearrange("p (t e) -> p t e", e=E)
        shifts = wide[:, 512:512 + E * TILES].rearrange("p (t e) -> p t e", e=E)
        gw_2 = gw[:, 4 * KD * D:]
        x_in = gw_2[:, 0:2 * UN * ROW].bitcast(F32).rearrange("p (s d) -> p s d", s=UN)
        table = gw_2[0:1, 2 * UN * ROW:2 * UN * ROW + 6 * TILES].bitcast(I32).rearrange(
            "p (a t) -> p a t", a=3)

        free = 2 * KD * N
        b3_in = tu[:, free:free + 2 * UN * F].bitcast(F32).rearrange("p (s f) -> p s f", s=UN)
        free += 2 * UN * F
        pad = tu[:, free:free + 2 * ROW].bitcast(F32)
        free += 2 * ROW
        x_part = tu[:, free:free + 2 * D].rearrange("p (h d) -> p h d", h=2)
        silu_h, gated, act_f = (rb[:, F * i:F * i + F] for i in range(3))
        act_part = rb[:, 3 * F:4 * F].bitcast(F16).rearrange("p (h f) -> p h f", h=2)
        y_out = rb[:, 4 * F:4 * F + UN * D].rearrange("p (s d) -> p s d", s=UN)

        psum = ctx.enter_context(nc.psum_tensor("psum", [P, 8, CW], F32))
        SUM = (0, 1)
        TP = (2, 3, 4, 5)
        UB = (6, 7)
        OT, XT, GATE, COUNT = (2, 3), (4, 5), 6, 7
        WARM = 0
        FA, FX, FY = (3, 4), 5, 6
        HG = ((0, NP - 1), (NP - 1, NP))

        small_in = sem("small_in")
        gw_arrived = [sem(f"gw_arrived{layer}") for layer in range(2)]
        x_arrived = [sem(f"x_arrived{c}") for c in range(NC)]
        row_arrived = [sem(f"row_arrived{r}") for r in range(TPC)]
        piece_arrived = [sem(f"piece_arrived{s}") for s in range(SLOTS_LATE)]
        xin_arrived = [sem(f"xin_arrived{s}") for s in range(UN)]
        b3_arrived = [sem(f"b3_arrived{s}") for s in range(UN)]
        consts, zeroed, late_consts = sem("consts"), sem("zeroed"), sem("late_consts")
        dve_step, pool_step = sem("dve_step"), sem("pool_step")
        var_1, std_1_ready, xn_act, bias_ready = sem("var_1"), sem("std_1_ready"), sem("xn_act"), sem("bias_ready")
        xn_dve = sem("xn_dve")
        gw_ready, scaled_1 = sem("gw_ready"), sem("scaled_1")
        xt_tp, xt_hi, xt_lo = sem("xt_tp"), sem("xt_hi"), sem("xt_lo")
        u_mm, u_hi, u_lo = sem("u_mm"), sem("u_hi"), sem("u_lo")
        adj_tp, adj_hi, adj_lo = sem("adj_tp"), sem("adj_hi"), sem("adj_lo")
        sum_mm, sum_read, h_parts, o_ready = sem("sum_mm"), sem("sum_read"), sem("h_parts"), sem("o_ready")
        o_tp, x_again, y_ready, y_stored = sem("o_tp"), sem("x_again"), sem("y_ready"), sem("y_stored")
        var_2, std_2_ready, row_ready = sem("var_2"), sem("std_2_ready"), sem("row_ready")
        row_copied = sem("row_copied")
        xn2_tp, xn2_copied, logits_mm = sem("xn2_tp"), sem("xn2_copied"), sem("logits_mm")
        gap_ready, exp_ready, mask_ready, rank_mm = sem("gap_ready"), sem("exp_ready"), sem("mask_ready"), sem("rank_mm")
        gate_read, slots_ready, weights_ready = sem("gate_read"), sem("slots_ready"), sem("weights_ready")
        scattered, carried = sem("scattered"), sem("carried")
        piece_hi, piece_lo = sem("piece_hi"), sem("piece_lo")
        count_mm, pads_known, table_ready = sem("count_mm"), sem("pads_known"), sem("table_ready")
        pad_built, pad_stored = sem("pad_built"), sem("pad_stored")
        token_read = sem("token_read")
        fx_tp, fx_hi, fx_lo = sem("fx_tp"), sem("fx_hi"), sem("fx_lo")
        hg_mm, silu_ready, gated_ready, act_ready = sem("hg_mm"), sem("silu_ready"), sem("gated_ready"), sem("act_ready")
        fa_tp, fa_hi, fa_lo = sem("fa_tp"), sem("fa_hi"), sem("fa_lo")
        fy_mm, fy_ready, fy_added, out_stored = sem("fy_mm"), sem("fy_ready"), sem("fy_added"), sem("out_stored")

        def ffn_tiles(eng, first_tile, tile, last_tile):
            first_tile()
            for t in range(1, UN):
                tile(t, t, 0, True, True)
            with eng.Fori(1, TILES // UN - 1) as i:
                for s in range(UN):
                    tile(i * UN + s, s, i, True, False)
            for t in range(TILES - UN, TILES):
                tile(t, t % UN, t // UN, t < TILES - 1, False)
            last_tile(TILES - 1, (TILES - 1) % UN)

        def expert_piece(e, n, part):
            mine = big[:, bass.ds(e * EW, EW)]
            if n < 2 * KD:
                v = mine[:, 0:W13].rearrange("p (k h m w) -> p k h m w", k=KD, h=2, m=NP)
                side = n // KD
                return v[:, n % KD, part, :, side * FP:(side + 1) * FP]
            v = mine[:, W13:].rearrange("p (f h d) -> p f h d", f=KF, h=2)
            half = n - 2 * KD
            return v[:, NP * half:NP * (half + 1), part, :]

        def acts(c, part, k):
            return act_t[:, bass.ds(c, 1), part, k, :].rearrange("p a w -> p (a w)")

        def load_piece(eng, e, n, m):
            dst = arriving(m)
            if n < 2 * KD:
                w, k = (w1, w3)[n // KD], n % KD
                src = w[bass.ds(e, 1), k * P:(k + 1) * P, :].rearrange("a p f -> (a p) f")
            else:
                h = n - 2 * KD
                src = w2[bass.ds(e, 1), h * NP * P:(h + 1) * NP * P, :].rearrange(
                    "a (f p) d -> (a p) f d", p=P)
                dst = dst.rearrange("p (f d) -> p f d", f=NP)
            eng.dma_start(dst, src).then_inc(piece_arrived[slot_of(m)[0]], 16)

        def load_last(eng, n):
            eng.wait_ge(piece_lo, split_before((E - 1) * PIECES + n))
            load_piece(eng, E - 1, n, (E - 1) * PIECES + n)

        def store_pad(eng, e):
            end = eng.value_load(pad_row[:, e:e + 1], min_val=e * REG, max_val=e * REG + N)
            eng.dma_start(routed[bass.ds(end, P), :], pad[:, :]).then_inc(pad_stored, 16)

        AHEAD = NT // 2 - 4

        def block_of(g, first):
            return (g % TPC, g // TPC) if first else (g // GPR, g % GPR)

        def start_order(normalize, transposed, times_w, block_0):
            normalize(0)
            normalize(1)
            transposed(0)
            normalize(2)
            transposed(1)
            times_w(0)
            times_w(1)
            normalize(3)
            transposed(2)
            times_w(2)
            times_w(3)
            transposed(3)
            for n in range(4, NT // 2):
                times_w(n)
                block_0(n - 4)

        block = ctx.enter_context(nc.Block())

        @block.sync
        def _(sp):
            for c in range(NC):
                sp.dma_start(x_all[:, TPC * c:TPC * (c + 1), :], x_t[:, TPC * c:TPC * (c + 1), :]
                             ).then_inc(x_arrived[c], 16)
            for r in range(TPC):
                sp.dma_start(adj_rows[r], adj[r * P:(r + 1) * P, :]).then_inc(row_arrived[r], 16)
            for r in range(TPC):
                sp.wait_ge(adj_tp, GPC - TPC + (r + 1))
                sp.dma_start(adj_rows[r], adj[(TPC + r) * P:(TPC + r + 1) * P, :]).then_inc(row_arrived[r], 16)
            with sp.Fori(2, NC) as c:
                for r in range(TPC):
                    sp.wait_ge(adj_tp, (c - 1) * GPC + (r + 1) * GPR)
                    sp.dma_start(adj_rows[r], adj[bass.ds((c * TPC + r) * P, P), :]
                                 ).then_inc(row_arrived[r], 16)

            sp.wait_ge(h_parts, KD * NC)
            for n in range(PIECES):
                if n == 2 * SLOTS - 1:
                    sp.wait_ge(o_ready, KD)
                if n >= SLOTS:
                    sp.wait_ge(piece_lo, n + 1 - SLOTS)
                load_piece(sp, 0, n, n)
            with sp.Fori(1, FEW_SLOTS // PIECES) as e:
                for n in range(PIECES):
                    sp.wait_ge(piece_lo, e * PIECES + (n + 1 - SLOTS))
                    load_piece(sp, e, n, PIECES + n)
            sp.wait_ge(o_ready, KD * (NC - 1))
            for m in range(FEW_SLOTS, (E - 1) * PIECES):
                sp.wait_ge(piece_lo, split_before(m))
                load_piece(sp, m // PIECES, m % PIECES, m)
            for n in range(LAST_BY_SP):
                load_last(sp, n)

            sp.wait_ge(pad_built, 1)
            sp.dma_start(total[N:N + P, :], pad[:, 0:D]).then_inc(pad_stored, 16)
            sp.wait_ge(pads_known, 1)
            for e in range(E):
                store_pad(sp, e)
            sp.wait_ge(table_ready, 1)

            def start_of(t):
                return sp.value_load(table[:, 0, bass.ds(t, 1)], min_val=0, max_val=E * REG - P)

            first_starts = [start_of(t) for t in range(UN)]
            sp.wait_ge(pad_stored, 16 * (E + 1))
            sp.wait_ge(scattered, 16 * NT * TOP)
            sp.wait_ge(y_stored, 16 * NC)

            def load_tile(s, start):
                sp.dma_start(x_in[:, s, :], routed[bass.ds(start, P), :]).then_inc(xin_arrived[s], 16)

            def load_b3(t, s):
                e = sp.value_load(table[:, 2, bass.ds(t, 1)], min_val=0, max_val=E - 1)
                sp.dma_start(b3_in[:, s, :], b3[bass.ds(e, 1), :].rearrange("a f -> (a f)").partition_broadcast(P)
                             ).then_inc(b3_arrived[s], 16)

            for t in range(UN):
                load_tile(t, first_starts[t])
            for t in range(UN):
                load_b3(t, t)
            with sp.Fori(1, TILES // UN) as i:
                for s in range(UN):
                    sp.wait_ge(fx_tp, (i - 1) * UN + (s + 1))
                    sp.wait_ge(token_read, (i - 1) * UN + (s + 1))
                    load_tile(s, start_of(i * UN + s))
                    sp.wait_ge(gated_ready, 2 * UN * (i - 1) + (2 * s + 2))
                    load_b3(i * UN + s, s)
            sp.wait_ge(fy_added, 16 * TILES)
            sp.dma_start(out.rearrange("(p t) d -> p (t d)", p=P), total[0:N, :].rearrange("(p t) d -> p (t d)", p=P)
                         ).then_inc(out_stored, 16)
            sp.wait_ge(out_stored, 16)

        @block.gpsimd
        def _(pool):
            step = Steps(pool, pool_step)
            nc.gpsimd.memset(ident[:], 0.0)
            nc.gpsimd.memset(ones[:], 1.0)
            nc.gpsimd.memset(carry, 0.0)
            nc.gpsimd.memset(eps, EPS)
            nc.gpsimd.iota(iota_e, pattern=[[1, E]], base=0, channel_multiplier=0,
                           allow_small_or_imprecise_dtypes=True)
            nc.gpsimd.iota(region_0, pattern=[[REG, E]], base=0, channel_multiplier=0,
                           allow_small_or_imprecise_dtypes=True)
            step.wait_for(nc.gpsimd.iota(token_no, pattern=[[P, NT]], base=0, channel_multiplier=1,
                                         allow_small_or_imprecise_dtypes=True))
            nc.gpsimd.affine_select(out=before[:], in_=ones[:], compare_op=ALU.is_gt, fill=0.0,
                                    base=0, pattern=[[1, P]], channel_multiplier=-1)
            nc.gpsimd.affine_select(out=ident[:], in_=ident[:], compare_op=ALU.not_equal, fill=1.0,
                                    base=0, pattern=[[-1, P]], channel_multiplier=1
                                    ).then_inc(consts, 1)
            raw_parts = gw_raw.rearrange("p (l k d) -> p l k d", l=2, k=2 * KD)
            for layer, k0, k1 in ((0, KD, 2 * KD), (0, 0, KD), (1, 0, 2 * KD)):
                if k0 != 0 or layer:
                    pool.wait_ge(gw_arrived[layer], 16)
                src = raw_parts[:, layer, k0:k1, :]
                hi, lo = (gwp[:, layer, part, k0:k1, :] for part in (HI, LO))
                step.wait_for(nc.gpsimd.tensor_scalar(src, src, S_W, None, ALU.mult))
                step.wait_for(nc.gpsimd.tensor_copy(hi, src))
                nc.gpsimd.tensor_tensor(lo, src, hi, ALU.subtract).then_inc(gw_ready, 1)
            pool.wait_ge(adj_tp, NC * GPC)
            nc.gpsimd.iota(iota_k, pattern=[[P, NT]], base=0, channel_multiplier=0,
                           allow_small_or_imprecise_dtypes=True)
            nc.gpsimd.iota(iota_n, pattern=[[1, TILES]], base=0, channel_multiplier=0,
                           allow_small_or_imprecise_dtypes=True)
            step.wait_for(nc.gpsimd.memset(upto, 1.0))
            nc.gpsimd.affine_select(out=upto, in_=upto, compare_op=ALU.is_ge, fill=0.0, base=0,
                                    pattern=[[1, E], [-1, E]], channel_multiplier=0
                                    ).then_inc(late_consts, 1)

            def scatter(c, first):
                if first:
                    pool.wait_ge(piece_lo, SLOTS)
                else:
                    pool.wait_ge(scattered, c * (16 * TPC * TOP))
                for k in range(TOP):
                    ins = nc.gpsimd.tensor_copy(row[k][:, :, D + 1], token_no[:, bass.ds(c * TPC, TPC)])
                step.wait_for(ins)
                pool.wait_ge(row_copied, c + 1)
                pool.wait_ge(slots_ready, c + 1)
                pool.wait_ge(weights_ready, c + 1)
                for q in range(TPC):
                    for k in range(TOP):
                        i = q * TOP + k
                        nc.gpsimd.indirect_dma_start(
                            out=routed, out_offset=bass.IndirectOffsetOnAxis(ap=slot[:, i:i + 1], axis=0),
                            in_=row[k][:, q, :], in_offset=None).then_inc(scattered, 16)

            for c in range(NC - 1):
                scatter(c, c == 0)

            pool.wait_ge(sum_mm, 2 * KD * NC)
            nc.gpsimd.iota(pad[:, D + 1:D + 2], pattern=[[0, 1]], base=N, channel_multiplier=1,
                           allow_small_or_imprecise_dtypes=True)
            nc.gpsimd.memset(pad[:, 0:D + 1], 0.0).then_inc(pad_built, 1)

            scatter(NC - 1, False)

            pool.wait_ge(y_stored, 16 * NC)
            pool.wait_ge(pad_stored, 16)
            for t in range(TILES):
                pool.wait_ge(fy_ready, t + 1)
                if t:
                    pool.wait_ge(fy_added, 16 * t)
                s = t % UN
                nc.gpsimd.indirect_dma_start(
                    out=total, out_offset=bass.IndirectOffsetOnAxis(ap=token_ix[:, s:s + 1], axis=0),
                    in_=y_out[:, s, :], in_offset=None, compute_op=ALU.add).then_inc(fy_added, 16)

        @block.tensor
        def _(pe):
            mm = nc.tensor.matmul
            pe.wait_ge(consts, 1)

            def x_chunk(c):
                pe.wait_ge(xn_dve, c + 1)
                pe.wait_ge(xn_act, c + 1)
                for k in range(KD):
                    n = KD * c + k
                    if n >= len(TP):
                        pe.wait_ge(xt_lo, n - len(TP) + 1)
                    for q in range(TPC):
                        last = nc.tensor.transpose(psum[:, TP[n % 4], q * P:(q + 1) * P],
                                                   xn_all[:, TPC * c + q, k * P:(k + 1) * P], ident[:])
                    last.then_inc(xt_tp, 1)

            def rows_times_w(layer, n):
                if layer == 0:
                    pe.wait_ge(xt_lo, KD * (n // 2 + 1))
                else:
                    pe.wait_ge(h_parts, KD * (n // 2 + 1))
                if n == 0:
                    pe.wait_ge(gw_ready, 1 if layer == 0 else 3)
                if layer or n >= 2:
                    pe.wait_ge(u_lo, layer * (NT // 2) + n - 1)
                for j in range(2):
                    jt = 2 * n + j
                    for i, (k, (a, b)) in enumerate((k, ab) for k in range(KD) for ab in PASSES):
                        last = mm(psum[:, UB[n % 2], j * D:(j + 1) * D],
                                  acts(jt // TPC, a, k)[:, (jt % TPC) * P:(jt % TPC + 1) * P], gwp[:, layer, b, KD + k, :],
                                  start=(i == 0), stop=(i == 3 * KD - 1))
                last.then_inc(u_mm, 1)

            def transpose_group(c, g, first):
                r, jq = block_of(g, first)
                if jq == 0:
                    pe.wait_ge(row_arrived[r], 16 * c + 16)
                if first and g < 4:
                    pe.wait_ge(xt_lo, KD * NC - 4 + g + 1)
                else:
                    pe.wait_ge(adj_lo, c * GPC + (g - 3))
                for b in range(JB):
                    j = JB * jq + b
                    last = nc.tensor.transpose(psum[:, TP[g % 4], b * P:(b + 1) * P],
                                               adj_rows[r][:, j * P:(j + 1) * P], ident[:])
                last.then_inc(adj_tp, 1)

            def chunk(layer, c, first, between):
                g = layer * NC + c
                if layer == 0:
                    pe.wait_ge(gw_ready, 2)
                for f in range(KD):
                    if not first:
                        pe.wait_ge(sum_read, KD * g + (f + 1 - KD))
                    for k in range(KD):
                        for i, (a, b) in enumerate(PASSES):
                            mm(psum[:, SUM[f], :], gwp[:, layer, a, k, f * P:(f + 1) * P],
                               acts(c, b, k), start=(k == 0 and i == 0), stop=False)
                pe.wait_ge(u_lo, (layer + 1) * (NT // 2))
                if layer == 0 and not first:
                    pe.wait_ge(adj_lo, c * GPC + GPC)
                for f in range(KD):
                    for j in range(NT):
                        if first and f == 0 and j % JB == 0:
                            pe.wait_ge(adj_lo, (j // JB + 1) * TPC)
                        for i, (a, b) in enumerate(PASSES):
                            last = mm(psum[:, SUM[f], :], u[:, a, j, f * P:(f + 1) * P],
                                      adj_t[:, bass.ds(c, 1), b, j, :].rearrange("p a w -> p (a w)"),
                                      start=False, stop=(j == NT - 1 and i == 2))
                        if j == NT - 1:
                            last.then_inc(sum_mm, 1)
                        for work in between.get((f, j), ()):
                            work()

            start_order(lambda c: None, x_chunk, lambda n: rows_times_w(0, n), lambda g: transpose_group(0, g, True))

            def with_next(c):
                return {(i // NT, i % NT): [lambda g=i // 2: transpose_group(c + 1, g, False)]
                        for i in range(0, KD * NT, 2)}

            beside = {(0, j): [] for j in range(GPC - AHEAD - 2)}
            for g in range(AHEAD, GPC):
                j = max(g - AHEAD - 2, (g - AHEAD) // 2)
                beside[(0, j)].append(lambda g=g: transpose_group(0, g, True))
            beside.update({(1, j): [lambda g=j: transpose_group(1, g, False)] for j in range(GPC)})
            chunk(0, 0, True, beside)
            with pe.Fori(1, NC - 1) as c:
                chunk(0, c, False, with_next(c))
            chunk(0, NC - 1, False, {})
            for n in range(NT // 2):
                rows_times_w(1, n)

            def o_back(c, first):
                pe.wait_ge(o_ready, KD * c + KD)
                for b in range(2):
                    if not first:
                        pe.wait_ge(y_ready, 2 * c + (b - 1))
                    for q in (2 * b, 2 * b + 1):
                        for f in range(KD):
                            at = (q % 2) * D + f * P
                            last = nc.tensor.transpose(psum[:, OT[b], at:at + P],
                                                       sum_2[:, f, q * P:(q + 1) * P], ident[:])
                    last.then_inc(o_tp, 1)

            def xn2_transposes(c):
                for b in range(2):
                    pe.wait_ge(row_ready, 2 * c + (b + 1))
                    for q in (2 * b, 2 * b + 1):
                        for k in range(KD):
                            at = (q % 2) * D + k * P
                            last = nc.tensor.transpose(psum[:, XT[b], at:at + P],
                                                       row[0][:, q, k * P:(k + 1) * P], ident[:])
                    last.then_inc(xn2_tp, 1)

            def gate_logits(c, first):
                if not first:
                    pe.wait_ge(gate_read, c)
                for q in range(TPC):
                    if q % 2 == 0:
                        pe.wait_ge(xn2_copied, 2 * c + (q // 2 + 1))
                    for k in range(KD):
                        last = mm(psum[:, GATE, q * E:(q + 1) * E], xn2_t[:, (q * KD + k) * P:(q * KD + k + 1) * P],
                                  wg_sb[:, k, :], start=(k == 0), stop=(k == KD - 1))
                last.then_inc(logits_mm, 1)

            def ranks(c):
                pe.wait_ge(mask_ready, c + 1)
                o = psum[:, GATE, 64:64 + TPC * E].rearrange("p (q e) -> p q e", q=TPC)
                mm(o, before[:], mask, start=True, stop=False)
                mm(o, ones[:], carry.unsqueeze(1).to_broadcast([P, TPC, E]), start=False, stop=False)
                for d in range(1, TPC):
                    last = mm(o[:, d:, :], ones[:], mask[:, 0:TPC - d, :], start=False, stop=(d == TPC - 1))
                last.then_inc(rank_mm, 1)

            def tail(c, first):
                return {(0, 0): [lambda: o_back(c, first)],
                        (0, 10): [lambda: xn2_transposes(c)],
                        (0, 15): [lambda: gate_logits(c, first)],
                        (1, 6): [lambda: ranks(c)]}

            chunk(1, 0, False, {})
            chunk(1, 1, False, tail(0, True))
            with pe.Fori(2, NC) as c:
                chunk(1, c, False, tail(c - 1, False))

            def keep_warm(n):
                for i in range(n):
                    mm(psum[:, WARM, :], ones[:], ones[:].unsqueeze(1).to_broadcast([P, CW // P, P]),
                       start=True, stop=True)

            o_back(NC - 1, False)
            keep_warm(22)
            xn2_transposes(NC - 1)
            gate_logits(NC - 1, False)
            keep_warm(6)
            pe.wait_ge(mask_ready, NC)
            pe.wait_ge(carried, NC - 1)
            mm(psum[:, COUNT, 0:E], ones[:], carry, start=True, stop=False)
            for q in range(TPC):
                last = mm(psum[:, COUNT, 0:E], ones[:], mask[:, q, :], start=False, stop=(q == TPC - 1))
            last.then_inc(count_mm, 1)
            ranks(NC - 1)

            def x_transposes(t, s, nth, first=False):
                pe.wait_ge(xin_arrived[s], 16 * nth + 16)
                if not first:
                    pe.wait_ge(fx_lo, t)
                for k in range(KD):
                    last = nc.tensor.transpose(psum[:, FX, k * P:(k + 1) * P],
                                               x_in[:, s, k * P:(k + 1) * P], ident[:])
                last.then_inc(fx_tp, 1)

            def hidden(t, place, m, first=False):
                if m == 0:
                    pe.wait_ge(fx_lo, t + 1)
                for i, (lo, _) in enumerate(HG):
                    if m == lo and not first:
                        pe.wait_ge(silu_ready, 2 * t + (i - 1))
                        pe.wait_ge(gated_ready, 2 * t + (i - 1))
                n = 0
                for k in range(KD):
                    for b, parts in ((HI, (HI, LO)), (LO, (HI,))):
                        w = big[:, bass.ds(place + ((k * 2 + b) * NP + m) * CW, CW)]
                        for a in parts:
                            last = mm(psum[:, m, :], x_part[:, a, k * P:(k + 1) * P], w,
                                      start=(n == 0), stop=(n == 3 * KD - 1))
                            n += 1
                if m + 1 in (HG[0][1], HG[1][1]):
                    last.then_inc(hg_mm, 1)

            def act_transposes(t, first=False):
                pe.wait_ge(act_ready, t + 1)
                for b, fs in enumerate((range(0, 4), range(4, KF))):
                    if not first:
                        pe.wait_ge(fa_lo, 2 * t + (b - 1))
                    for f in fs:
                        last = nc.tensor.transpose(psum[:, FA[b], (f % 4) * P:(f % 4 + 1) * P],
                                                   act_f[:, f * P:(f + 1) * P], ident[:])
                    last.then_inc(fa_tp, 1)

            def down(t, place, first=False):
                if not first:
                    pe.wait_ge(fy_ready, t)
                n = 0
                for f in range(KF):
                    if f == 0:
                        pe.wait_ge(fa_lo, 2 * t + 1)
                    if f == 4:
                        pe.wait_ge(fa_lo, 2 * t + 2)
                    for b, parts in ((HI, (HI, LO)), (LO, (HI,))):
                        w = big[:, bass.ds(place + (W13 + (f * 2 + b) * D), D)]
                        for a in parts:
                            last = mm(psum[:, FY, 0:D], act_part[:, a, f * P:(f + 1) * P], w,
                                      start=(n == 0), stop=(n == 3 * KF - 1))
                            n += 1
                last.then_inc(fy_mm, 1)

            def place_of(t):
                return pe.value_load(table[:, 1, bass.ds(t, 1)], min_val=0, max_val=(E - 1) * EW)

            def first_tile():
                pe.wait_ge(table_ready, 1)
                pe.wait_ge(piece_lo, E * PIECES - 4)
                keep_warm(14)
                p = place_of(0)
                pe.wait_ge(piece_lo, E * PIECES)
                x_transposes(0, 0, 0, first=True)
                for m in range(NP):
                    hidden(0, p, m, first=True)
                x_transposes(1, 1, 0)

            def tile(t, s, nth, more, fresh):
                p = place_of(t)
                hidden(t, p, 0)
                act_transposes(t - 1, first=isinstance(t, int) and t == 1)
                hidden(t, p, 1)
                hidden(t, p, 2)
                if more:
                    s1 = (s + 1) % UN
                    x_transposes(t + 1, s1, nth + (1 if s1 == 0 else 0))
                down(t - 1, place_of(t - 1))

            def last_tile(t, s):
                act_transposes(t)
                down(t, place_of(t))

            ffn_tiles(pe, first_tile, tile, last_tile)

        @block.scalar
        def _(act):
            def ln_std(out_ap, var_ap):
                return nc.scalar.activation(out_ap, var_ap, ACT.Sqrt, bias=eps)

            def high(dst, src, scale):
                return nc.scalar.activation(dst, src, ACT.Copy, scale=scale)

            def table_load(function):
                nc.scalar.activation(scratch, eps, function)

            act.wait_ge(consts, 1)
            table_load(ACT.Sqrt)
            raw_w = gw_raw.rearrange("p (l k d) -> p l k d", l=2, k=2 * KD)
            for layer, w in enumerate((gnn_w1, gnn_w2)):
                act.dma_start(raw_w[:, layer, :, :], w.rearrange("(k p) d -> p k d", p=P)).then_inc(gw_arrived[layer], 16)
            with nc.allow_non_contiguous_dma(reason="two short bias vectors and the gate"):
                for layer, b in enumerate((gnn_b1, gnn_b2)):
                    act.dma_start(bias[:, layer, :], b.rearrange("(k p) -> p k", p=P)).then_inc(small_in, 16)
                act.dma_start(wg_sb, wg.rearrange("(k p) e -> p k e", p=P)).then_inc(small_in, 16)
            def normalize(c):
                ts = slice(TPC * c, TPC * (c + 1))
                act.wait_ge(var_1, c + 1)
                ln_std(std_1[:, ts], mv_1[:, ts, 1]).then_inc(std_1_ready, 1)
                act.wait_ge(scaled_1, c + 1)
                for t in range(TPC * c + TPC // 2, TPC * (c + 1)):
                    ins = nc.scalar.activation(xn_all[:, t, :], x_all[:, t, :], ACT.Identity,
                                               scale=rstd_1[:, t:t + 1], bias=shift_1[:, t:t + 1])
                ins.then_inc(xn_act, 1)

            def x_high_1(c):
                for k in range(KD):
                    n = KD * c + k
                    act.wait_ge(xt_tp, n + 1)
                    high(acts(c, HI, k), psum[:, TP[n % 4], :], S_ACT).then_inc(xt_hi, 1)

            def u_high(layer, n):
                act.wait_ge(u_mm, layer * (NT // 2) + n + 1)
                high(u[:, HI, 2 * n:2 * n + 2, :].rearrange("p j d -> p (j d)"), psum[:, UB[n % 2], :],
                     S_ACT / S_SUM).then_inc(u_hi, 1)

            def block_high(c, g, first=False):
                r, jq = block_of(g, first)
                act.wait_ge(adj_tp, c * GPC + (g + 1))
                high(adj_t[:, bass.ds(c, 1), HI, JB * jq:JB * (jq + 1), r * P:(r + 1) * P].rearrange(
                         "p a j w -> p (a j) w"),
                     psum[:, TP[g % 4], :].rearrange("p (j w) -> p j w", j=JB), S_W).then_inc(adj_hi, 1)

            def relu_1(c, f, first):
                if not first:
                    act.wait_ge(h_parts, KD * c + (f + 1 - KD))
                act.wait_ge(sum_mm, KD * c + (f + 1))
                nc.scalar.activation(sum_1[:, f, :], psum[:, SUM[f], :], ACT.Relu, scale=S_ACT / S_SUM,
                                     bias=bias_h[:, f:f + 1]).then_inc(sum_read, 1)

            start_order(normalize, x_high_1, lambda n: u_high(0, n), lambda g: block_high(0, g, True))

            def layer_1(c, first, more):
                for f in range(KD):
                    if more:
                        for g in range(f * GPC // 2, (f + 1) * GPC // 2):
                            block_high(c + 1, g)
                    relu_1(c, f, first)

            for g in range(AHEAD, GPC):
                block_high(0, g, True)
            act.wait_ge(bias_ready, 1)
            relu_1(0, 0, True)
            for g in range(GPC):
                block_high(1, g)
            relu_1(0, 1, True)
            act.wait_ge(gw_ready, 3)
            with act.Fori(1, NC - 1) as c:
                layer_1(c, False, True)
            layer_1(NC - 1, False, False)
            for n in range(NT // 2):
                u_high(1, n)

            def relu_2(c, f):
                act.wait_ge(sum_mm, KD * c + (KD * NC + f + 1))
                nc.scalar.activation(sum_2[:, f, :], psum[:, SUM[f], :], ACT.Relu, scale=1.0 / S_SUM,
                                     bias=bias[:, 1, f:f + 1]).then_inc(sum_read, 1)

            def load_x(c):
                act.dma_start(y_ch, x_t[:, bass.ds(c * TPC, TPC), :]).then_inc(x_again, 16)

            def piece_high(m):
                slot, nth = slot_of(m)
                act.wait_ge(piece_arrived[slot], 16 * nth)
                high(expert_piece(m // PIECES, m % PIECES, HI),
                     arriving(m).rearrange("p (a d) -> p a d", a=NP), S_W).then_inc(piece_hi, 1)

            def tail(c, more, cuts):
                def pieces(i):
                    for m in range(([0] + cuts)[i], cuts[i]):
                        piece_high(SPLIT[c] + m)
                        n = SPLIT[c] + m + (SLOTS_LATE - 2) - (E - 1) * PIECES
                        if LAST_BY_SP <= n < PIECES:
                            load_last(act, n)

                act.wait_ge(var_2, c + 1)
                ln_std(std_2, mv_2[:, :, 1]).then_inc(std_2_ready, 1)
                act.wait_ge(y_ready, 2 * c + 2)
                act.dma_start(total_t[:, TPC * c:TPC * (c + 1), :], y_ch).then_inc(y_stored, 16)
                pieces(0)
                for b in range(2):
                    act.wait_ge(xn2_tp, 2 * c + (b + 1))
                    nc.scalar.copy(xn2_t[:, b * CW:(b + 1) * CW], psum[:, XT[b], :]).then_inc(xn2_copied, 1)
                act.wait_ge(row_ready, 2 * c + 2)
                nc.scalar.copy(row[1][:, :, 0:D], row[0][:, :, 0:D]).then_inc(row_copied, 1)
                table_load(ACT.Exp)
                pieces(1)
                if more:
                    act.wait_ge(y_stored, 16 * c + 16)
                    load_x(c + 1)
                    act.wait_ge(logits_mm, c + 1)
                    relu_2(c + 1, 0)
                act.wait_ge(gap_ready, c + 1)
                nc.scalar.activation(expd, gap, ACT.Exp).then_inc(exp_ready, 1)
                pieces(2)
                if more:
                    relu_2(c + 1, 1)
                pieces(3)
                if more:
                    table_load(ACT.Sqrt)

            act.wait_ge(adj_tp, NC * GPC)
            load_x(0)
            for m in range(SPLIT[0]):
                piece_high(m)
            for f in range(KD):
                relu_2(0, f)
            table_load(ACT.Sqrt)
            for c in range(NC):
                n = SPLIT[c + 1] - SPLIT[c]
                more = c < NC - 1
                tail(c, more, [3, 6, n - 1, n] if more else [3, 4, n, n])
            table_load(ACT.Silu)

            def x_high(t):
                act.wait_ge(fx_tp, t + 1)
                high(x_part[:, HI, :], psum[:, FX, 0:D], S_ACT).then_inc(fx_hi, 1)

            def silu(t, first=False):
                if not first:
                    act.wait_ge(act_ready, t)
                for i, (lo, hi) in enumerate(HG):
                    act.wait_ge(hg_mm, 2 * t + (i + 1))
                    nc.scalar.activation(silu_h[:, lo * FP:hi * FP].rearrange("p (m w) -> p m w", w=FP),
                                         psum[:, lo:hi, 0:FP], ACT.Silu, scale=1.0 / S_SUM
                                         ).then_inc(silu_ready, 1)

            def act_high(t):
                for b, (lo, hi) in enumerate(((0, CW), (CW, F))):
                    act.wait_ge(fa_tp, 2 * t + (b + 1))
                    high(act_part[:, HI, lo:hi], psum[:, FA[b], 0:hi - lo], 1.0).then_inc(fa_hi, 1)

            def first_tile():
                x_high(0)
                silu(0, first=True)
                x_high(1)

            def tile(t, s, nth, more, fresh):
                act_high(t - 1)
                silu(t)
                if more:
                    x_high(t + 1)

            ffn_tiles(act, first_tile, tile, lambda t, s: act_high(t))

        @block.vector
        def _(dve):
            step = Steps(dve, dve_step)
            v = nc.vector

            def low(dst, src, scale, hi_part):
                return v.scalar_tensor_tensor(out=dst, in0=src, scalar=scale, in1=hi_part,
                                              op0=ALU.mult, op1=ALU.subtract)

            def layernorm_stats(src, st, mv, n):
                for q in range(n):
                    ins = v.bn_stats(st[:, q, :], src[:, q, :])
                step.wait_for(ins)
                for q in range(n):
                    ins = v.bn_aggr(mv[:, q, :], st[:, q, :])
                return ins

            def stats(c):
                ts = slice(TPC * c, TPC * (c + 1))
                dve.wait_ge(x_arrived[c], 16)
                layernorm_stats(x_all[:, ts, :], st_1[:, ts, :], mv_1[:, ts, :], TPC).then_inc(var_1, 1)

            def normalize(c):
                ts = slice(TPC * c, TPC * (c + 1))
                dve.wait_ge(std_1_ready, c + 1)
                step.wait_for(v.reciprocal(rstd_1[:, ts], std_1[:, ts]))
                v.scalar_tensor_tensor(out=shift_1[:, ts], in0=mv_1[:, ts, 0], scalar=-1.0, in1=rstd_1[:, ts],
                                       op0=ALU.mult, op1=ALU.mult).then_inc(scaled_1, 1)
                for t in range(TPC * c, TPC * c + TPC // 2):
                    ins = v.tensor_scalar(xn_all[:, t, :], x_all[:, t, :], mv_1[:, t, 0:1], rstd_1[:, t:t + 1],
                                          ALU.subtract, ALU.mult)
                ins.then_inc(xn_dve, 1)
                if c + 1 < NC:
                    stats(c + 1)

            def x_low_1(c):
                for k in range(KD):
                    n = KD * c + k
                    dve.wait_ge(xt_hi, n + 1)
                    low(acts(c, LO, k), psum[:, TP[n % 4], :], S_ACT, acts(c, HI, k)).then_inc(xt_lo, 1)

            def u_low(layer, n):
                dve.wait_ge(u_hi, layer * (NT // 2) + n + 1)
                low(u[:, LO, 2 * n:2 * n + 2, :].rearrange("p j d -> p (j d)"), psum[:, UB[n % 2], :],
                    S_ACT / S_SUM, u[:, HI, 2 * n:2 * n + 2, :].rearrange("p j d -> p (j d)")
                    ).then_inc(u_lo, 1)

            def block_low(c, g, first=False):
                r, jq = block_of(g, first)
                dve.wait_ge(adj_hi, c * GPC + (g + 1))
                hi, lo = (adj_t[:, bass.ds(c, 1), h, JB * jq:JB * (jq + 1), r * P:(r + 1) * P].rearrange(
                    "p a j w -> p (a j) w") for h in (HI, LO))
                low(lo, psum[:, TP[g % 4], :].rearrange("p (j w) -> p j w", j=JB), S_W, hi).then_inc(adj_lo, 1)

            def h_split(c, f):
                dve.wait_ge(sum_read, KD * c + (f + 1))
                step.wait_for(v.tensor_copy(acts(c, HI, f), sum_1[:, f, :]))
                v.tensor_tensor(acts(c, LO, f), sum_1[:, f, :], acts(c, HI, f),
                                ALU.subtract).then_inc(h_parts, 1)

            stats(0)
            start_order(normalize, x_low_1, lambda n: u_low(0, n), lambda g: block_low(0, g, True))

            def layer_1(c, more):
                for f in range(KD):
                    if more:
                        for g in range(f * GPC // 2, (f + 1) * GPC // 2):
                            block_low(c + 1, g)
                    h_split(c, f)

            for g in range(AHEAD, GPC):
                block_low(0, g, True)
            dve.wait_ge(small_in, 48)
            v.tensor_scalar(bias_h, bias[:, 0, :], S_ACT, None, ALU.mult).then_inc(bias_ready, 1)
            h_split(0, 0)
            for g in range(GPC):
                block_low(1, g)
            h_split(0, 1)
            dve.wait_ge(gw_ready, 3)
            base = step.n
            with dve.Fori(1, NC - 1) as c:
                step.base, step.n = base + (c - 1) * KD, 0
                layer_1(c, True)
            step.base, step.n = base + (NC - 2) * KD, 0
            layer_1(NC - 1, False)
            for n in range(NT // 2):
                u_low(1, n)

            def add_h(c, f):
                dve.wait_ge(sum_read, KD * c + (KD * NC + f + 1))
                step.wait_for(v.scalar_tensor_tensor(
                    out=sum_2[:, f, :], in0=acts(c, LO, f), scalar=1.0 / S_ACT, in1=sum_2[:, f, :],
                    op0=ALU.mult, op1=ALU.add))
                v.scalar_tensor_tensor(
                    out=sum_2[:, f, :], in0=acts(c, HI, f), scalar=1.0 / S_ACT, in1=sum_2[:, f, :],
                    op0=ALU.mult, op1=ALU.add).then_inc(o_ready, 1)

            def piece_low(m):
                dve.wait_ge(piece_hi, m + 1)
                low(expert_piece(m // PIECES, m % PIECES, LO), arriving(m).rearrange("p (a d) -> p a d", a=NP),
                    S_W, expert_piece(m // PIECES, m % PIECES, HI)).then_inc(piece_lo, 1)

            def tail(c, first, more, cuts):
                def pieces(i):
                    for m in range(([0] + cuts)[i], cuts[i]):
                        piece_low(SPLIT[c] + m)

                pieces(0)
                dve.wait_ge(x_again, 16 * c + 16)
                for b in range(2):
                    dve.wait_ge(o_tp, 2 * c + (b + 1))
                    y2 = y_ch[:, 2 * b:2 * b + 2, :].rearrange("p q d -> p (q d)")
                    v.scalar_tensor_tensor(out=y2, in0=psum[:, OT[b], :], scalar=0.0, in1=y2,
                                           op0=ALU.max, op1=ALU.add).then_inc(y_ready, 1)
                dve.wait_ge(y_ready, 2 * c + 2)
                layernorm_stats(y_ch, st_2, mv_2, TPC).then_inc(var_2, 1)
                pieces(1)
                dve.wait_ge(std_2_ready, c + 1)
                step.wait_for(v.reciprocal(rstd_2, std_2))
                if not first:
                    dve.wait_ge(scattered, c * (16 * TPC * TOP))
                for q in range(TPC):
                    ins = v.tensor_scalar(row[0][:, q, 0:D], y_ch[:, q, :], mv_2[:, q, 0:1], rstd_2[:, q:q + 1],
                                          ALU.subtract, ALU.mult)
                    if q % 2:
                        ins.then_inc(row_ready, 1)
                pieces(2)
                dve.wait_ge(logits_mm, c + 1)
                step.wait_for(v.tensor_copy(logits, psum[:, GATE, 0:TPC * E].rearrange("p (q e) -> p q e", q=TPC)))
                for q in range(TPC):
                    ins = v.max(best[:, q, :], logits[:, q, :])
                step.wait_for(ins)
                v.tensor_tensor(gap, best[:, :, 1], best[:, :, 0], ALU.subtract).then_inc(gap_ready, 1)
                for q in range(TPC):
                    ins = v.max_index(best_ix[:, q, :], best[:, q, :], logits[:, q, :])
                step.wait_for(ins)
                step.wait_for(v.tensor_copy(choice, best_ix[:, :, 0:TOP]))
                pick = small["choice"].unsqueeze(2).to_broadcast([P, TPC * TOP, E])
                step.wait_for(v.tensor_tensor(
                    small["onehot"].rearrange("p (i e) -> p i e", e=E), pick,
                    iota_e.unsqueeze(1).to_broadcast([P, TPC * TOP, E]), ALU.is_equal))
                v.tensor_tensor(mask, onehot[:, :, 0, :], onehot[:, :, 1, :], ALU.add).then_inc(mask_ready, 1)
                pieces(3)
                dve.wait_ge(exp_ready, c + 1)
                step.wait_for(v.tensor_scalar(den, expd, 1.0, None, ALU.add))
                step.wait_for(v.reciprocal(row[0][:, :, D], den))
                v.tensor_tensor(row[1][:, :, D], expd, row[0][:, :, D], ALU.mult).then_inc(weights_ready, 1)
                if not more:
                    dve.wait_ge(count_mm, 1)
                    step.wait_for(v.tensor_copy(n_e, psum[0:1, COUNT, 0:E]))
                    step.wait_for(v.tensor_tensor(pad_f, n_e, region_0[0:1, :], ALU.add))
                    v.tensor_copy(pad_row, pad_f).then_inc(pads_known, 1)
                dve.wait_ge(rank_mm, c + 1)
                v.tensor_tensor(place, psum[:, GATE, 64:64 + TPC * E].rearrange("p (q e) -> p q e", q=TPC),
                                region_0.unsqueeze(1).to_broadcast([P, TPC, E]), ALU.add).then_inc(gate_read, 1)
                if more:
                    with nc.allow_low_precision(reason="counts up to 16"):
                        step.wait_for(v.tensor_reduce(added, mask.rearrange("p q e -> p e q"), AX_X, ALU.add))
                    v.tensor_tensor(carry, carry, added, ALU.add).then_inc(carried, 1)
                dve.wait_ge(gate_read, c + 1)
                for k in range(TOP):
                    ins = v.tensor_tensor(picked[:, :, k, :], onehot[:, :, k, :], place, ALU.mult)
                step.wait_for(ins)
                step.wait_for(v.tensor_reduce(slot_f, small["picked"].rearrange("p (i e) -> p i e", e=E),
                                              AX_X, ALU.add))
                v.tensor_copy(slot, slot_f).then_inc(slots_ready, 1)
                if more:
                    pieces(4)
                    add_h(c + 1, 0)
                    pieces(5)
                    add_h(c + 1, 1)
                    pieces(6)

            for m in range(SPLIT[0]):
                piece_low(m)
            for f in range(KD):
                add_h(0, f)
            for c in range(NC):
                n = SPLIT[c + 1] - SPLIT[c]
                tail(c, c == 0, c < NC - 1, [0, 0, 4, 6, n - 2, n - 1, n] if c < NC - 1 else [0, 0, 3, 3])

            dve.wait_ge(late_consts, 1)
            step.wait_for(v.tensor_tensor(over_k, n_e.unsqueeze(2).to_broadcast([1, E, NT]),
                                          iota_k.unsqueeze(1).to_broadcast([1, E, NT]), ALU.is_gt))
            step.wait_for(v.tensor_reduce(nt_e, over_k, AX_X, ALU.add))
            v.memset(delta[:, 0:1], 0.0)
            v.tensor_scalar(delta[:, 1:E], nt_e[:, 0:E - 1], -float(P), float(REG), ALU.mult, ALU.add)
            step.wait_for(v.tensor_tensor(over_e, nt_e.unsqueeze(1).to_broadcast([1, E, E]), upto, ALU.mult))
            step.wait_for(v.tensor_reduce(last, over_e, AX_X, ALU.add))
            step.wait_for(v.tensor_tensor(first, last, nt_e, ALU.subtract))
            piece_low(SPLIT[NC - 1] + 3)
            piece_low(SPLIT[NC - 1] + 4)
            step.wait_for(v.tensor_tensor(started, iota_n.unsqueeze(2).to_broadcast([1, TILES, E]),
                                          first.unsqueeze(1).to_broadcast([1, TILES, E]), ALU.is_ge))
            v.tensor_reduce(experts_seen, started, AX_X, ALU.add)
            step.wait_for(v.tensor_tensor(shifts, started, delta.unsqueeze(1).to_broadcast([1, TILES, E]), ALU.mult))
            step.wait_for(v.tensor_reduce(row_shift, shifts, AX_X, ALU.add))
            step.wait_for(v.scalar_tensor_tensor(out=tab_f[:, 0, :], in0=iota_n, scalar=float(P), in1=row_shift,
                                                 op0=ALU.mult, op1=ALU.add))
            v.tensor_scalar(tab_f[:, 0, :], tab_f[:, 0, :], pad_f[:, E - 1:E], None, ALU.min)
            v.tensor_scalar(tab_f[:, 1, :], experts_seen, float(EW), -float(EW), ALU.mult, ALU.add)
            step.wait_for(v.tensor_scalar(tab_f[:, 2, :], experts_seen, -1.0, None, ALU.add))
            v.tensor_copy(table, tab_f).then_inc(table_ready, 1)
            for m in range(5, SPLIT[NC] - SPLIT[NC - 1]):
                piece_low(SPLIT[NC - 1] + m)

            def token_copy(t, s, nth, fresh):
                dve.wait_ge(xin_arrived[s], 16 * nth + 16)
                if not fresh:
                    dve.wait_ge(fy_added, 16 * t + 16 * (1 - UN))
                v.tensor_copy(token_w[:, s:s + 1], x_in[:, s, D:D + 1])
                v.tensor_copy(token_ix[:, s:s + 1], x_in[:, s, D + 1:D + 2]).then_inc(token_read, 1)

            def x_low(t):
                dve.wait_ge(fx_hi, t + 1)
                low(x_part[:, LO, :], psum[:, FX, 0:D], S_ACT, x_part[:, HI, :]).then_inc(fx_lo, 1)

            def gate_g(t, s, nth):
                dve.wait_ge(b3_arrived[s], 16 * nth + 16)
                for i, (lo, hi) in enumerate(HG):
                    dve.wait_ge(silu_ready, 2 * t + (i + 1))
                    v.scalar_tensor_tensor(out=gated[:, lo * FP:hi * FP].rearrange("p (m w) -> p m w", w=FP),
                                           in0=psum[:, lo:hi, FP:2 * FP], scalar=1.0 / S_SUM,
                                           in1=b3_in[:, s, lo * FP:hi * FP].rearrange(
                                               "p (m w) -> p m w", w=FP), op0=ALU.mult, op1=ALU.add
                                           ).then_inc(gated_ready, 1)

            def activate(t, first=False):
                dve.wait_ge(gated_ready, 2 * t + 2)
                if not first:
                    dve.wait_ge(fa_tp, 2 * t)
                v.scalar_tensor_tensor(out=act_f, in0=gated, scalar=S_ACT, in1=silu_h,
                                       op0=ALU.mult, op1=ALU.mult).then_inc(act_ready, 1)

            def act_low(t):
                for b, (lo, hi) in enumerate(((0, CW), (CW, F))):
                    dve.wait_ge(fa_hi, 2 * t + (b + 1))
                    v.tensor_tensor(act_part[:, LO, lo:hi], psum[:, FA[b], 0:hi - lo], act_part[:, HI, lo:hi],
                                    ALU.subtract).then_inc(fa_lo, 1)

            def y_weigh(t, s):
                dve.wait_ge(fy_mm, t + 1)
                dve.wait_ge(token_read, t + 1)
                v.tensor_scalar(y_out[:, s, :], psum[:, FY, 0:D], token_w[:, s:s + 1], 1.0 / S_SUM,
                                ALU.mult, ALU.mult).then_inc(fy_ready, 1)

            def first_tile():
                dve.wait_ge(table_ready, 1)
                x_low(0)
                token_copy(0, 0, 0, fresh=True)
                gate_g(0, 0, 0)
                x_low(1)
                activate(0, first=True)

            def tile(t, s, nth, more, fresh):
                act_low(t - 1)
                token_copy(t, s, nth, fresh)
                gate_g(t, s, nth)
                if more:
                    x_low(t + 1)
                activate(t)
                y_weigh(t - 1, (s - 1) % UN)

            def last_tile(t, s):
                act_low(t)
                y_weigh(t, s)

            ffn_tiles(dve, first_tile, tile, last_tile)


_INS = ['x', 'adj', 'L0_gnn_W1', 'L0_gnn_b1', 'L0_gnn_W2', 'L0_gnn_b2', 'L0_ffn_Wg', 'L0_ffn_W1',
        'L0_ffn_W2', 'L0_ffn_W3', 'L0_ffn_b3']
_OUTS = [((2048, 256), 'float32')]


def kernel(**inputs):
    import numpy as _np
    import concourse.bacc as _bacc
    from concourse import mybir as _mybir
    from concourse.bass_utils import run_bass_kernel_spmd as _run

    nc = _bacc.Bacc("TRN2", target_bir_lowering=False, num_devices=1)
    arrays, args = {}, []
    for name in _INS:
        a = _np.ascontiguousarray(inputs[name])
        arrays[f"in_{name}_dram"] = a
        args.append(nc.dram_tensor(f"in_{name}_dram", a.shape, _mybir.dt.from_np(a.dtype), kind="ExternalInput").ap())
    for i, (shape, dtype) in enumerate(_OUTS):
        dt = _mybir.dt.from_np(_np.dtype(dtype))
        args.append(nc.dram_tensor(f"out_{i}_dram", shape, dt, kind="ExternalOutput").ap())
    moe_gnn_kernel(nc, *args)
    r = _run(nc, [arrays], core_ids=[0])
    got = tuple(r.results[0][f"out_{i}_dram"] for i in range(len(_OUTS)))
    return got[0]
```
